# Optimizing a Trainium2 kernel written in Bass

```python
import numpy as np
import jax
import jax.numpy as jnp

def _softmax(x, axis=-1):
    return jax.nn.softmax(x, axis=axis)

def _gelu(x):
    return jax.nn.gelu(x, approximate=True)

def _silu(x):
    return jax.nn.silu(x)

def _sigmoid(x):
    return jax.nn.sigmoid(x)

def _layernorm(x, axis=-1, eps=1e-05):
    m = jnp.mean(x, axis=axis, keepdims=True)
    v = jnp.var(x, axis=axis, keepdims=True)
    return (x - m) / jnp.sqrt(v + eps)

def _scatter_add(tgt, idx, src, axis=0):
    return tgt.at[idx].add(src)

def _segment_sum(src, seg, n):
    return jax.ops.segment_sum(src, seg, n)
kernel_name = 'mk_seq_preln_d1_jaxref_r4_3aadac'

def setup_inputs(seed: int=0):
    np.random.seed(seed)
    _w = jnp.asarray

    def _L0_attn_setup():
        import jax, jax.numpy as jnp
        import numpy as np
        B, S, D = (4, 256, 512)
        H, G = (16, 2)
        HD = D // H

        def rotate_half(x):
            x1, x2 = (x[..., :x.shape[-1] // 2], x[..., x.shape[-1] // 2:])
            return jnp.concatenate([-x2, x1], axis=-1)
        key = jax.random.key(seed)
        ks = jax.random.split(key, 9)
        scale = 0.02
        return {'x': jax.random.normal(ks[0], (B, S, D), jnp.float32), 'wq': jax.random.normal(ks[1], (D, D), jnp.float32) * scale, 'bq': jnp.zeros((D,), jnp.float32), 'wk': jax.random.normal(ks[2], (D, G * HD), jnp.float32) * scale, 'bk': jnp.zeros((G * HD,), jnp.float32), 'wv': jax.random.normal(ks[3], (D, G * HD), jnp.float32) * scale, 'bv': jnp.zeros((G * HD,), jnp.float32), 'wo': jax.random.normal(ks[4], (D, D), jnp.float32) * scale, 'bo': jnp.zeros((D,), jnp.float32)}
    _L0_attn_in = _L0_attn_setup()

    def _L0_ffn_setup():
        import jax, jax.numpy as jnp
        import numpy as np
        E4M3_MAX = 448.0

        def _quant_e4m3(t):
            amax = jnp.max(jnp.abs(t)).astype(jnp.float32)
            scale = jnp.maximum(amax / E4M3_MAX, 1e-12)
            fp8 = (t.astype(jnp.float32) / scale).astype(jnp.float8_e4m3fn)
            return (fp8, scale)

        def _scaled_mm(a_fp8, b_fp8, sa, sb):
            acc = jnp.matmul(a_fp8.astype(jnp.float32), b_fp8.astype(jnp.float32))
            return (acc * (sa * sb)).astype(jnp.bfloat16)
        key = jax.random.key(seed)
        k1, k2 = jax.random.split(key)
        x = jax.random.normal(k1, (4, 512, 512), dtype=jnp.bfloat16)
        weight = (jax.random.normal(k2, (512, 512), dtype=jnp.bfloat16) * 0.02).astype(jnp.bfloat16)
        return {'x': x, 'weight': weight}
    _L0_ffn_in = _L0_ffn_setup()
    _d = {'L0_attn_x': _L0_attn_in['x'], 'L0_attn_wq': _L0_attn_in['wq'], 'L0_attn_bq': _L0_attn_in['bq'], 'L0_attn_wk': _L0_attn_in['wk'], 'L0_attn_bk': _L0_attn_in['bk'], 'L0_attn_wv': _L0_attn_in['wv'], 'L0_attn_bv': _L0_attn_in['bv'], 'L0_attn_wo': _L0_attn_in['wo'], 'L0_attn_bo': _L0_attn_in['bo'], 'L0_ffn_weight': _L0_ffn_in['weight']}
    _x0 = _d['L0_attn_x']
    _d['L0_attn_x'] = jax.random.normal(jax.random.fold_in(jax.random.key(seed), 1), (2, 2048, 512), dtype=_x0.dtype)
    del _x0
    return _d

def reference(L0_attn_x, L0_attn_wq, L0_attn_bq, L0_attn_wk, L0_attn_bk, L0_attn_wv, L0_attn_bv, L0_attn_wo, L0_attn_bo, L0_ffn_weight):

    def _L0_attn_ref(x, wq, bq, wk, bk, wv, bv, wo, bo):
        import jax, jax.numpy as jnp
        import numpy as np
        B, S, D = (4, 256, 512)
        H, G = (16, 2)
        HD = D // H

        def rotate_half(x):
            x1, x2 = (x[..., :x.shape[-1] // 2], x[..., x.shape[-1] // 2:])
            return jnp.concatenate([-x2, x1], axis=-1)
        b, s, d = x.shape
        hd = HD
        q = (x @ wq + bq).reshape(b, s, H, hd)
        k = (x @ wk + bk).reshape(b, s, G, hd)
        v = (x @ wv + bv).reshape(b, s, G, hd)
        inv_freq = 1.0 / 2500 ** (jnp.arange(0, hd, 2, dtype=jnp.float32) / hd)
        t = jnp.arange(s, dtype=jnp.float32)
        freqs = jnp.outer(t, inv_freq)
        freqs = jnp.concatenate([freqs, freqs], -1)
        sin = jnp.sin(freqs)[:, None, :]
        cos = jnp.cos(freqs)[:, None, :]
        q = q * cos + rotate_half(q) * sin
        q = q * hd ** (-0.5)
        k = k * cos + rotate_half(k) * sin
        reps = H // G
        k_exp = jnp.repeat(k, reps, axis=2)
        v_exp = jnp.repeat(v, reps, axis=2)
        scores = jnp.einsum('bqhd,bkhd->bhqk', q, k_exp) * hd ** (-0.5)
        attn = jax.nn.softmax(scores, axis=-1)
        out = jnp.einsum('bhqk,bkhd->bqhd', attn, v_exp).reshape(b, s, d)
        return out @ wo + bo

    def _L0_ffn_ref(x, weight):
        import jax, jax.numpy as jnp
        import numpy as np
        E4M3_MAX = 448.0

        def _quant_e4m3(t):
            amax = jnp.max(jnp.abs(t)).astype(jnp.float32)
            scale = jnp.maximum(amax / E4M3_MAX, 1e-12)
            fp8 = (t.astype(jnp.float32) / scale).astype(jnp.float8_e4m3fn)
            return (fp8, scale)

        def _scaled_mm(a_fp8, b_fp8, sa, sb):
            acc = jnp.matmul(a_fp8.astype(jnp.float32), b_fp8.astype(jnp.float32))
            return (acc * (sa * sb)).astype(jnp.bfloat16)
        w_fp8, w_scale = _quant_e4m3(weight)
        x2d = x.reshape(-1, x.shape[-1])
        x_fp8, x_scale = _quant_e4m3(x2d)
        out2d = _scaled_mm(x_fp8, w_fp8.T, x_scale, w_scale)
        return out2d.reshape(*x.shape[:-1], out2d.shape[-1])
    x = L0_attn_x
    x = x + _L0_attn_ref(_layernorm(x, axis=-1), L0_attn_wq, L0_attn_bq, L0_attn_wk, L0_attn_bk, L0_attn_wv, L0_attn_bv, L0_attn_wo, L0_attn_bo)
    x = x + _L0_ffn_ref(_layernorm(x, axis=-1), L0_ffn_weight)
    return x

_drawn_inputs = setup_inputs


def setup_inputs(seed=0):
    import zlib

    import numpy as np

    out = dict(_drawn_inputs(seed))
    spreads = {'L0_attn_bq': (0.0, 0.8),
     'L0_attn_bk': (0.0, 0.8),
     'L0_attn_bv': (0.0, 0.1),
     'L0_attn_bo': (0.0, 0.1)}
    factors = {'L0_attn_wq': 8.0, 'L0_attn_wk': 8.0, 'L0_attn_wv': 8.0}
    for name, (base, spread) in spreads.items():
        noise = np.random.default_rng([zlib.crc32(name.encode()), seed]).standard_normal(out[name].shape)
        drawn = base * np.exp(spread * noise) if base else spread * noise
        out[name] = jnp.asarray(drawn.astype(out[name].dtype))
    for name, factor in factors.items():
        out[name] = (out[name] * factor).astype(out[name].dtype)
    return out
```

```python
from contextlib import ExitStack, contextmanager

import numpy as np

import concourse.bass as bass
from concourse import mybir

F32 = mybir.dt.float32
F32R = mybir.dt.float32r
BF16 = mybir.dt.bfloat16
U32 = mybir.dt.uint32
ALU = mybir.AluOpType
ACT = mybir.ActivationFunctionType
AX = mybir.AxisListType
ds = bass.ds

P = 128
EPS = 1e-5
E4M3_MAX = 448.0


class Steps:

    def __init__(self, eng, sem):
        self.eng, self.sem, self.base, self.k = eng, sem, 0, 0

    def did(self, ins):
        ins.then_inc(self.sem, 1)
        self.k += 1

    def settle(self):
        self.eng.wait_ge(self.sem, self.base + self.k)

    @contextmanager
    def loop(self, count, per):
        base, k = self.base, self.k
        with self.eng.Fori(0, count) as i:
            self.base, self.k = base + k + i * per, 0
            yield i
            assert self.k == per, (self.k, per)
        self.base, self.k = base, k + count * per


def layer(nc, x, wq, bq, wk, bk, wv, bv, wo, bo, w_ffn, rope_cos, rope_sin, out):
    B, S, D = x.shape
    HD = rope_cos.shape[1]
    H, G = wq.shape[1] // HD, wk.shape[1] // HD
    KC = D // P
    NT = S // P
    T_ALL = B * NT
    QB = 512
    NQ = S // QB
    TQ = QB // P
    HG = H // G
    QUAD = P // HD
    NQUAD = HG // QUAD
    NC = S // P
    SUM = 4
    KVW = 2 * G * HD
    QKW = D + G * HD
    NR = QKW // HD
    SHIFT_ROW = 3 * HD
    SCALE = 1.0 / HD
    M_LIMIT = 40.0
    assert KC == 4 and QUAD == 4 and NQUAD == 2 and D == 512 and G == 2

    x_t = x.rearrange("b (t p) d -> p (b t) d", p=P)
    out_t = out.rearrange("b (t p) d -> (b t) p d", p=P)

    with ExitStack() as ctx:
        def sb(name, shape, dt):
            return ctx.enter_context(nc.sbuf_tensor(name, shape, dt))

        def psum(name, shape, dt):
            return ctx.enter_context(nc.psum_tensor(name, shape, dt))

        def sem(name):
            return ctx.enter_context(nc.semaphore(name))

        xs = sb("xs", [P, T_ALL, D], F32)
        w_in = sb("w_in", [P, KC, D + KVW], F32)
        w_out = sb("w_out", [P, KC, D], F32)
        w_ffn_rows = sb("w_ffn_rows", [P, KC, D], BF16)
        w_ffn_t = sb("w_ffn_t", [P, KC, D], BF16)
        b_in = sb("b_in", [P, D + KVW], F32)
        b_out = sb("b_out", [P, D], F32)
        cos_t = sb("cos_t", [P, NT, HD], F32)
        sin_t = sb("sin_t", [P, NT, HD], F32)
        ident = sb("ident", [P, P], F32)
        ident_bf = sb("ident_bf", [P, P], BF16)
        ones = sb("ones", [P, HD], F32)
        q_rot = sb("q_rot", [P, G * NT * HG * HD], F32)
        k_stack = sb("k_stack", [P, G, S], F32R)
        k_cur = sb("k_cur", [P, S], F32R)
        v_all = sb("v_all", [P, NT, G * HD], F32)
        v_cur = sb("v_cur", [P, NT, HD], F32)
        q_stack = sb("q_stack", [P, HG, QB], F32R)
        work = sb("work", [P, 6144], F32)
        recip = sb("recip", [P, QB], F32)
        neg_max = sb("neg_max", [P, SHIFT_ROW + 16], F32)
        stats = sb("stats", [P, T_ALL, 6], F32)
        mom = sb("mom", [P, 8, T_ALL], F32)
        amax = sb("amax", [P, 2, T_ALL], F32)
        norm2 = sb("norm2", [P, NR], F32)
        norm2_max = sb("norm2_max", [P, NR], F32)
        bound = sb("bound", [P, 10], F32)
        shift = sb("shift", [P, 1], F32)
        small = sb("small", [1, 1], mybir.dt.int32)
        one_row = sb("one_row", [P, 1], F32)
        plus_half = sb("plus_half", [P, 2], F32)
        half = sb("half", [P, T_ALL], F32)
        sc = sb("sc", [P, 16], F32)
        spare = sb("spare", [P, 16], F32)

        expo = work[:, 0:4096].rearrange("p (s n) -> p s n", s=4)
        sums = work[:, 4096:6144]
        xn = work[:, 0:1024].rearrange("p (u n) -> p u n", u=2)
        xnt = work[:, 1024:2048].rearrange("p (u k n) -> p u k n", u=2, k=KC)
        qk_raw = work[:, 2048:2048 + QKW]
        rot_a = work[:, 2624:2624 + QKW]
        rot_b = work[:, 3200:3200 + QKW]
        k_split = work[:, 4096:5120].rearrange("p (t g n) -> p t g n", t=4, g=G)
        q_split = work[:, 4096:6144].rearrange("p (u h n) -> p u h n", u=2, h=HG)
        att_tile = work[:, 0:1024].rearrange("p (u k n) -> p u k n", u=2, k=KC)
        y = work[:, 0:512]
        y_pow = work[:, 512:1024]
        y_sum = work[:, 3840:4352]
        y_q = work[:, 1024:1536].bitcast(BF16).rearrange("p (u n) -> p u n", u=2)
        y_t = work[:, 1792:2304].bitcast(BF16).rearrange("p (u k n) -> p u k n", u=2, k=KC)
        ffn_bf = work[:, 2304:2816].bitcast(BF16).rearrange("p (u n) -> p u n", u=2)
        final = work[:, 2816:3840].rearrange("p (u n) -> p u n", u=2)

        S_ps = [psum(f"s_ps{i}", [P, 2 * QB], F32) for i in range(2)]
        acc_ps = psum("acc_ps", [P, QB], F32)
        den_ps = psum("den_ps", [P, QB], F32)
        X_ps = [psum(f"x_ps{i}", [P, QB], F32) for i in range(2)]

        x_landed = sem("x_landed")
        w_landed = sem("w_landed")
        pool_step = sem("pool_step")
        dve_step = sem("dve_step")
        act_step = sem("act_step")
        consts_made = sem("consts_made")
        w_amax = sem("w_amax")
        w_amax_all = sem("w_amax_all")
        w_quantised = sem("w_quantised")
        w_turned = sem("w_turned")
        w_stored = sem("w_stored")
        var_ready = sem("var_ready")
        rstd_ready = sem("rstd_ready")
        norm_ready = sem("norm_ready")
        bias_added = sem("bias_added")
        norms_ready = sem("norms_ready")
        norms_all = sem("norms_all")
        root_ready = sem("root_ready")
        bound_ready = sem("bound_ready")
        k_copied = sem("k_copied")
        waited = sem("waited")
        k_made = sem("k_made")
        xn_ready = sem("xn_ready")
        xn_turned = sem("xn_turned")
        xnt_stored = sem("xnt_stored")
        projected = sem("projected")
        proj_read = sem("proj_read")
        tile_rotated = sem("tile_rotated")
        k_turned = sem("k_turned")
        k_stored = sem("k_stored")
        kv_current = sem("kv_current")
        q_parted = sem("q_parted")
        q_turned = sem("q_turned")
        q_stored = sem("q_stored")
        pre_scores = sem("pre_scores")
        pre_maxed = sem("pre_maxed")
        pre_turned = sem("pre_turned")
        neg_ready = sem("neg_ready")
        rows_ready = sem("rows_ready")
        shift_stored = sem("shift_stored")
        scores_ready = sem("scores_ready")
        exp_done = sem("exp_done")
        pv_done = sem("pv_done")
        adds_done = sem("adds_done")
        sums_used = sem("sums_used")
        acc_ready = sem("acc_ready")
        att_stored = sem("att_stored")
        att_copied = sem("att_copied")
        att_projected = sem("att_projected")
        res_added = sem("res_added")
        y_amax = sem("y_amax")
        y_amax_all = sem("y_amax_all")
        y_ready = sem("y_ready")
        y_turned = sem("y_turned")
        yt_stored = sem("yt_stored")
        ffn_done = sem("ffn_done")
        ffn_scaled = sem("ffn_scaled")
        final_ready = sem("final_ready")
        stats_done = sem("stats_done")
        stats2_done = sem("stats2_done")
        out_stored = [sem(f"out_stored{u}") for u in range(2)]
        W_ALL = 16 * 11
        block = ctx.enter_context(nc.Block())

        def exp_no(n, c, s):
            return n * (2 * NC) + (2 * c + s + 1)

        ADDS = 2 * (SUM - 1)

        def adds_no(n, c, s):
            return n * (NC // SUM * ADDS) + (c // SUM * ADDS + 2 * (c % SUM - 1) + s + 1)

        @block.sync
        def _(sp):
            def load_x(b):
                for c in range(4):
                    t = b * NT + c * (NT // 4)
                    sp.dma_start(xs[:, t:t + NT // 4, :], x_t[:, t:t + NT // 4, :]).then_inc(x_landed, 16)

            load_x(0)
            sp.dma_start(w_in[:, :, 0:D], wq.rearrange("(c p) n -> p c n", p=P)).then_inc(w_landed, 16)
            sp.dma_start(w_in[:, :, D:D + G * HD], wk.rearrange("(c p) n -> p c n", p=P)).then_inc(w_landed, 16)
            sp.dma_start(w_in[:, :, D + G * HD:D + KVW], wv.rearrange("(c p) n -> p c n", p=P)).then_inc(w_landed, 16)
            sp.dma_start(b_in[:, 0:D], bq.partition_broadcast(P)).then_inc(w_landed, 16)
            sp.dma_start(b_in[:, D:D + G * HD], bk.partition_broadcast(P)).then_inc(w_landed, 16)
            sp.dma_start(b_in[:, D + G * HD:D + KVW], bv.partition_broadcast(P)).then_inc(w_landed, 16)
            sp.dma_start(b_out[:], bo.partition_broadcast(P)).then_inc(w_landed, 16)
            sp.dma_start(cos_t[:], rope_cos.rearrange("(t p) n -> p t n", p=P)).then_inc(w_landed, 16)
            sp.dma_start(sin_t[:], rope_sin.rearrange("(t p) n -> p t n", p=P)).then_inc(w_landed, 16)
            sp.dma_start(w_ffn_rows[:], w_ffn.rearrange("(c p) n -> p c n", p=P)).then_inc(w_landed, 16)
            sp.dma_start(w_out[:], wo.rearrange("(c p) n -> p c n", p=P)).then_inc(w_landed, 16)
            sp.wait_ge(x_landed, 64)
            load_x(1)
            with sp.Fori(0, T_ALL // 2) as tp:
                for u in range(2):
                    sp.wait_ge(final_ready, tp * 2 + u + 3)
                    sp.dma_start(out_t[ds(tp * 2 + u, 1)].rearrange("a p d -> (a p) d"),
                                 final[:, u]).then_inc(out_stored[u], 16)
            for u in range(2):
                sp.wait_ge(out_stored[u], 16 + 16 * (T_ALL // 2))

        @block.gpsimd
        def _(pool):
            step = Steps(pool, pool_step)
            step.did(pool.memset(ident[:], 0.0))
            step.did(pool.memset(half[:], -0.5))
            step.did(pool.memset(plus_half[:], 0.5))
            step.settle()
            step.did(pool.affine_select(out=ident[:], in_=ident[:], compare_op=ALU.not_equal, fill=1.0,
                                        base=0, pattern=[[-1, P]], channel_multiplier=1))
            step.settle()
            pool.tensor_copy(ident_bf[:], ident[:]).then_inc(consts_made, 1)
            pool.wait_ge(w_landed, W_ALL)
            pool.wait_ge(w_amax, 1)
            pool.partition_all_reduce(sc[:, 1:2], sc[:, 0:1], P, bass.bass_isa.ReduceOp.max)\
                .then_inc(w_amax_all, 1)
            with pool.Fori(0, B) as b:
                pool.wait_ge(var_ready, b + 1)
                pool.tensor_tensor(mom[:, 2, ds(b * NT, NT)], mom[:, 1, ds(b * NT, NT)], half[:, 0:NT], ALU.pow)\
                    .then_inc(rstd_ready, 1)
                pool.wait_ge(rstd_ready, b + 1)
                pool.tensor_tensor(mom[:, 7, ds(b * NT, NT)], mom[:, 0, ds(b * NT, NT)],
                                   mom[:, 2, ds(b * NT, NT)], ALU.mult).then_inc(norm_ready, 1)
                with pool.Fori(0, NT) as t:
                    pool.wait_ge(xn_ready, b * NT + t + 1)
                    tile = xs[:, ds(b * NT + t, 1), :].rearrange("p a d -> p (a d)")
                    pool.tensor_tensor(tile, tile, b_out[:], ALU.add).then_inc(bias_added, 1)
                pool.wait_ge(norms_ready, b + 1)
                pool.sem_inc(waited, 1)
                pool.partition_all_reduce(bound[:, 2:4], bound[:, 0:2], P, bass.bass_isa.ReduceOp.max)\
                    .then_inc(norms_all, 1)
                pool.wait_ge(norms_all, b + 1)
                pool.tensor_tensor(bound[:, 4:6], bound[:, 2:4], plus_half[:], ALU.pow).then_inc(root_ready, 1)
            pool.wait_ge(var_ready, B + 1)
            pool.tensor_tensor(mom[:, 2, :], mom[:, 1, :], half[:], ALU.pow).then_inc(rstd_ready, 1)
            pool.wait_ge(y_amax, 1)
            pool.partition_all_reduce(sc[:, 9:10], sc[:, 8:9], P, bass.bass_isa.ReduceOp.max)\
                .then_inc(y_amax_all, 1)

        @block.vector
        def _(dve):
            step = Steps(dve, dve_step)

            def quantise(dst):
                step.did(dve.tensor_scalar(y_pow.bitcast(U32), y.bitcast(U32), 0x7F800000, None, ALU.bitwise_and))
                step.settle()
                step.did(dve.tensor_scalar(y_pow, y_pow, 2.0 ** -6, 1.5 * 2.0 ** 20, ALU.max, ALU.mult))
                step.settle()
                step.did(dve.tensor_tensor(y_sum, y, y_pow, ALU.add))
                step.settle()
                return dve.tensor_tensor(dst, y_sum, y_pow, ALU.subtract)

            def scales(col):
                step.did(dve.tensor_scalar(sc[:, col + 1:col + 2], sc[:, col:col + 1], 1.0 / E4M3_MAX, 1e-12,
                                           ALU.mult, ALU.max))
                step.settle()
                step.did(dve.reciprocal(sc[:, col + 2:col + 3], sc[:, col + 1:col + 2]))
                step.settle()

            def moments(first, n):
                st = lambda k: stats[:, ds(first, n), k:k + 1].rearrange("p t a -> p (t a)")
                m = lambda k: mom[:, k, ds(first, n)]
                step.did(dve.tensor_tensor(m(0), st(1), st(4), ALU.add))
                step.did(dve.tensor_tensor(m(3), st(1), st(4), ALU.subtract))
                step.did(dve.tensor_tensor(m(4), st(2), st(5), ALU.add))
                step.settle()
                step.did(dve.tensor_scalar(m(0), m(0), -0.5, None, ALU.mult))
                step.did(dve.tensor_tensor(m(5), m(3), m(3), ALU.mult))
                step.did(dve.tensor_scalar(m(4), m(4), 1.0 / D, EPS, ALU.mult, ALU.add))
                step.settle()
                return dve.scalar_tensor_tensor(out=m(1), in0=m(5), scalar=0.25, in1=m(4),
                                                op0=ALU.mult, op1=ALU.add)

            for k, (signal, n) in enumerate([
                    (proj_read, 1), (att_stored, 1), (res_added, 2), (xn_turned, 2), (y_turned, 2),
                    (ffn_scaled, 2), (final_ready, 2), (out_stored[0], 16), (out_stored[1], 16), (k_turned, 1), (k_stored, 2),
                    (att_projected, 2)]):
                dve.memset(spare[:, k:k + 1], 0.0).then_inc(signal, n)
            step.did(dve.memset(ones[:], 1.0))
            step.did(dve.memset(neg_max[:], 0.0))
            step.did(dve.memset(one_row[:], 0.0))
            step.settle()
            step.did(dve.memset(one_row[SHIFT_ROW:SHIFT_ROW + 1, :], 1.0))

            dve.wait_ge(w_landed, W_ALL)
            dve.tensor_reduce(sc[:, 0:1], w_ffn_rows[:].rearrange("p c n -> p (c n)"), AX.X, ALU.max,
                              apply_absolute_value=True).then_inc(w_amax, 1)
            dve.wait_ge(w_amax_all, 1)
            scales(1)
            for c in range(KC):
                if c >= 2:
                    dve.wait_ge(w_turned, c - 1)
                step.did(dve.tensor_scalar(y, w_ffn_rows[:, c, :], sc[:, 3:4], None, ALU.mult))
                step.settle()
                quantise(y_q[:, c % 2]).then_inc(w_quantised, 1)
                dve.wait_ge(w_quantised, c + 1)

            BATCH = 6 + 1 + 10 * NT + 5 + (G * NQ) * (TQ + NQUAD)

            def twice(a, h):
                return a[:, :, None, :].broadcast_to([P, h, 2, HD])

            with step.loop(B, BATCH) as b:
                with dve.Fori(0, NT) as t:
                    dve.wait_ge(x_landed, (b + 1) * 64)
                    dve.bn_stats(stats[:, ds(b * NT + t, 1), :].rearrange("p a k -> p (a k)"),
                                 xs[:, ds(b * NT + t, 1), :].rearrange("p a d -> p (a d)"))\
                        .then_inc(stats_done, 1)
                dve.wait_ge(stats_done, b * NT + NT)
                moments(b * NT, NT).then_inc(var_ready, 1)

                step.did(dve.memset(norm2_max[:], 0.0))
                step.settle()
                dve.sem_inc(waited, 1)
                with step.loop(NT // 4, 4 * 10) as t4:
                  for tt in range(4):
                    t = t4 * 4 + tt
                    T = b * NT + t
                    dve.wait_ge(projected, T + 1)
                    step.did(dve.tensor_tensor(qk_raw, S_ps[1][:, 0:QKW], b_in[:, 0:QKW], ALU.add))
                    dve.tensor_tensor(v_all[:, ds(t, 1), :].rearrange("p a n -> p (a n)"),
                                      S_ps[1][:, QKW:D + KVW], b_in[:, QKW:D + KVW], ALU.add)\
                        .then_inc(proj_read, 1)
                    step.settle()
                    heads = lambda a: a.rearrange("p (h n) -> p h n", n=HD)
                    step.did(dve.tensor_tensor(rot_a, qk_raw, qk_raw, ALU.mult))
                    step.settle()
                    step.did(dve.tensor_reduce(norm2[:, 0:NR], heads(rot_a), AX.X, ALU.add))
                    step.settle()
                    step.did(dve.tensor_tensor(norm2_max[:], norm2_max[:], norm2[:, 0:NR], ALU.max))
                    cos_b = cos_t[:, ds(t, 1), :].broadcast_to([P, NR, HD])
                    step.did(dve.tensor_tensor(heads(rot_a), heads(qk_raw), cos_b, ALU.mult))
                    for s in range(2):
                        h0, h1 = s * (HD // 2), (1 - s) * (HD // 2)
                        sin_b = sin_t[:, ds(t, 1), h0:h0 + HD // 2].broadcast_to([P, NR, HD // 2])
                        step.did(dve.tensor_tensor(heads(rot_b)[:, :, h0:h0 + HD // 2],
                                                   heads(qk_raw)[:, :, h1:h1 + HD // 2], sin_b, ALU.mult))
                    step.settle()
                    step.did(dve.tensor_tensor(
                        q_rot[:].rearrange("p (g t n) -> p g t n", g=G, t=NT)[:, :, ds(t, 1), :]
                        .rearrange("p g a n -> p g (a n)"),
                        rot_a[:, 0:D].rearrange("p (g n) -> p g n", g=G),
                        rot_b[:, 0:D].rearrange("p (g n) -> p g n", g=G), ALU.add))
                    step.did(dve.tensor_tensor(qk_raw[:, D:QKW], rot_a[:, D:QKW], rot_b[:, D:QKW], ALU.add))
                    step.settle()
                    ks = k_split[:, tt].rearrange("p g (r s n) -> p g r s n", r=2, s=2)
                    k_new = heads(qk_raw[:, D:QKW])
                    if tt == 0:
                        dve.wait_ge(k_turned, b * (NT // 4) + t4 + 1)
                    step.did(dve.tensor_copy(ks[:, :, :, 0, :].bitcast(F32R), twice(k_new, G)))
                    step.settle()
                    dve.tensor_tensor(ks[:, :, :, 1, :], twice(k_new, G), ks[:, :, :, 0, :], ALU.subtract)\
                        .then_inc(tile_rotated, 1)
                    dve.wait_ge(tile_rotated, T + 1)

                step.settle()
                step.did(dve.tensor_reduce(bound[:, 0:1], norm2_max[:, 0:H], AX.X, ALU.max))
                step.settle()
                dve.tensor_reduce(bound[:, 1:2], norm2_max[:, H:NR], AX.X, ALU.max).then_inc(norms_ready, 1)
                dve.wait_ge(root_ready, b + 1)
                step.did(dve.scalar_tensor_tensor(out=bound[:, 6:7], in0=bound[:, 4:5], scalar=1.001 * SCALE,
                                                  in1=bound[:, 5:6], op0=ALU.mult, op1=ALU.mult))
                step.settle()
                step.did(dve.tensor_scalar(bound[:, 7:8], bound[:, 6:7], M_LIMIT, None, ALU.is_le))
                step.did(dve.tensor_scalar(bound[:, 8:9], bound[:, 6:7], M_LIMIT, -1.0, ALU.min, ALU.mult))
                step.settle()
                step.did(dve.tensor_tensor(shift[:], bound[:, 7:8], bound[:, 8:9], ALU.mult))
                step.settle()
                dve.tensor_copy(small[:], bound[0:1, 7:8]).then_inc(bound_ready, 1)
                dve.wait_ge(bound_ready, b + 1)
                dve.sem_inc(waited, 1)
                general = dve.value_load(small[0:1, 0:1], min_val=0, max_val=1) < 1
                with step.loop(G * NQ, TQ + NQUAD) as f:
                    F = b * (G * NQ) + f
                    dve.wait_ge(att_stored, F * NQUAD + 1)
                    dve.wait_ge(k_turned, (b + 1) * (NT // 4) + 1)
                    for tt in range(TQ):
                        u = tt % 2
                        qs = q_split[:, u].rearrange("p h (s r n) -> p h s r n", s=2, r=2)
                        q_new = q_rot[:, ds((f * TQ + tt) * (HG * HD), HG * HD)].rearrange("p (h n) -> p h n", h=HG)
                        if tt >= 2:
                            dve.wait_ge(q_turned, F * TQ + tt - 1)
                        step.did(dve.tensor_copy(qs[:, :, 0].bitcast(F32R), twice(q_new, HG)))
                        step.settle()
                        dve.tensor_tensor(qs[:, :, 1], twice(q_new, HG), qs[:, :, 0],
                                          ALU.subtract).then_inc(q_parted, 1)
                    with dve.If(general):
                        with dve.Fori(0, NQUAD) as i:
                            n = F * NQUAD + i
                            for c in range(NC):
                                for s in range(2):
                                    dve.wait_ge(pre_scores, exp_no(n, c, s))
                                    top = sums[:, s * 1024:s * 1024 + 1024]
                                    if c == 0:
                                        dve.wait_ge(q_turned, F * TQ + TQ)
                                        dve.tensor_copy(top, S_ps[s][:]).then_inc(pre_maxed, 1)
                                    else:
                                        dve.wait_ge(pre_maxed, exp_no(n, c - 1, s))
                                        dve.tensor_tensor(top, S_ps[s][:], top, ALU.max).then_inc(pre_maxed, 1)
                            dve.wait_ge(pre_turned, n + 1)
                            for s in range(2):
                                dve.tensor_reduce(neg_max[:, SHIFT_ROW + 8 * s:SHIFT_ROW + 8 * s + 8],
                                                  S_ps[s][:].rearrange("p (e n) -> p e n", e=8), AX.X, ALU.max,
                                                  negate=True).then_inc(neg_ready, 1)
                    with dve.Else():
                        dve.sem_inc(pre_maxed, NQUAD * 2 * NC)
                        dve.sem_inc(neg_ready, NQUAD * 2)
                    with step.loop(NQUAD, 1) as i:
                        n = F * NQUAD + i
                        for c in range(NC):
                            if c % SUM == 0:
                                continue
                            for s in range(2):
                                add = sums[:, s * 1024:s * 1024 + 1024]
                                dve.wait_ge(exp_done, exp_no(n, c, s))
                                if c % SUM == 1:
                                    if c // SUM:
                                        dve.wait_ge(sums_used, n * (NC // SUM - 1) + c // SUM)
                                    a = expo[:, (2 * (c - 1) + s) % 4]
                                else:
                                    dve.wait_ge(adds_done, adds_no(n, c - 1, s))
                                    a = add
                                dve.tensor_tensor(add, a, expo[:, (2 * c + s) % 4], ALU.add)\
                                    .then_inc(adds_done, 1)
                        dve.wait_ge(acc_ready, n + 1)
                        step.did(dve.reciprocal(recip[:], den_ps[:]))
                        step.settle()
                        dve.tensor_tensor(q_rot[:, ds((f * NQUAD + i) * QB, QB)], acc_ps[:], recip[:], ALU.mult)\
                            .then_inc(att_stored, 1)

                with dve.Fori(0, NT // 2) as tp:
                    for u in range(2):
                        T = b * NT + tp * 2 + u
                        tile = lambda: xs[:, ds(T, 1), :].rearrange("p a d -> p (a d)")
                        dve.wait_ge(att_projected, T + 3)
                        dve.wait_ge(bias_added, T + 1)
                        dve.tensor_tensor(tile(), X_ps[u][:], tile(), ALU.add).then_inc(res_added, 1)
                        dve.wait_ge(res_added, T + 3)
                        dve.bn_stats(stats[:, ds(T, 1), :].rearrange("p a k -> p (a k)"), tile()).then_inc(stats2_done, 1)
                        dve.tensor_reduce(amax[:, 0, ds(T, 1)], tile(), AX.X, ALU.max).then_inc(stats2_done, 1)
                        dve.tensor_reduce(amax[:, 1, ds(T, 1)], tile(), AX.X, ALU.min).then_inc(stats2_done, 1)

            dve.wait_ge(stats2_done, 3 * T_ALL)
            moments(0, T_ALL).then_inc(var_ready, 1)
            dve.wait_ge(var_ready, B + 1)
            for k in range(2):
                step.did(dve.tensor_tensor(amax[:, k, :], amax[:, k, :], mom[:, 0, :], ALU.add))
            dve.wait_ge(rstd_ready, B + 1)
            step.settle()
            for k in range(2):
                step.did(dve.tensor_tensor(amax[:, k, :], amax[:, k, :], mom[:, 2, :], ALU.mult))
            step.settle()
            dve.tensor_reduce(sc[:, 8:9], amax[:].rearrange("p k t -> p (k t)"), AX.X, ALU.max,
                              apply_absolute_value=True).then_inc(y_amax, 1)
            dve.wait_ge(y_amax_all, 1)
            scales(9)
            step.did(dve.tensor_tensor(sc[:, 12:13], sc[:, 10:11], sc[:, 2:3], ALU.mult))
            step.did(dve.tensor_scalar(mom[:, 6, :], mom[:, 2, :], sc[:, 11:12], None, ALU.mult))
            step.settle()
            with step.loop(T_ALL // 2, 2 * 4) as tp:
                for u in range(2):
                    T = tp * 2 + u
                    tile = lambda: xs[:, ds(T, 1), :].rearrange("p a d -> p (a d)")
                    step.did(dve.tensor_scalar(y, tile(), mom[:, 0, ds(T, 1)], mom[:, 6, ds(T, 1)],
                                               ALU.add, ALU.mult))
                    step.settle()
                    dve.wait_ge(y_turned, T + 1)
                    quantise(y_q[:, u]).then_inc(y_ready, 1)
                    dve.wait_ge(y_ready, T + 1)
                    dve.wait_ge(ffn_scaled, T + 3)
                    dve.wait_ge(out_stored[u], tp * 16 + 16)
                    dve.tensor_tensor(final[:, u], tile(), ffn_bf[:, u], ALU.add).then_inc(final_ready, 1)

        @block.scalar
        def _(act):
            act.wait_ge(proj_read, 1)
            act.activation(spare[:, 15:16], spare[:, 0:1], ACT.Exp).then_inc(act_step, 1)
            for c in range(KC):
                act.wait_ge(w_turned, c + 1)
                act.activation(w_ffn_t[:, :, c * P:(c + 1) * P],
                               X_ps[c % 2][:].bitcast(BF16)[:, 0:D].rearrange("p (k n) -> p k n", k=KC),
                               ACT.Copy).then_inc(w_stored, 1)
            with act.Fori(0, B) as b:
                with act.Fori(0, NT // 4) as t4:
                    act.wait_ge(norm_ready, b + 1)
                    act.wait_ge(att_stored, b * (G * NQ * NQUAD) + 1)
                    act.wait_ge(res_added, b * NT + 1)
                    for tt in range(4):
                        u = tt % 2
                        T = b * NT + t4 * 4 + tt
                        act.wait_ge(xn_turned, T + 1)
                        act.activation(xn[:, u], xs[:, ds(T, 1), :].rearrange("p a d -> p (a d)"), ACT.Identity,
                                       bias=mom[:, 7, ds(T, 1)], scale=mom[:, 2, ds(T, 1)]).then_inc(xn_ready, 1)
                        act.wait_ge(xn_turned, b * NT + t4 * 4 + tt + 3)
                        act.activation(xnt[:, u].rearrange("p k n -> p (k n)"), S_ps[0][:, u * D:(u + 1) * D],
                                       ACT.Copy).then_inc(xnt_stored, 1)
                    act.wait_ge(k_turned, b * (NT // 4) + t4 + 2)
                    for u in range(2):
                        act.activation(
                            k_stack[:, :, ds(t4 * QB + u * 2 * P, 2 * P)].rearrange("p g (t n) -> p t g n", t=2),
                            X_ps[u][:].rearrange("p (t g n) -> p t g n", t=2, g=G), ACT.Copy)\
                            .then_inc(k_stored, 1)
                act.wait_ge(bound_ready, b + 1)
                act.sem_inc(waited, 1)
                general = act.value_load(small[0:1, 0:1], min_val=0, max_val=1) < 1
                with act.Fori(0, G) as g:
                    act.wait_ge(k_stored, (b + 1) * (NT // 2) + 2)
                    act.wait_ge(proj_read, (b + 1) * NT + 1)
                    act.wait_ge(att_stored, (b * G + g) * (NQ * NQUAD) + 1)
                    act.activation(k_cur[:], k_stack[:, ds(g, 1), :].rearrange("p a n -> p (a n)").bitcast(F32),
                                   ACT.Copy).then_inc(k_copied, 1)
                    act.wait_ge(k_copied, b * G + g + 1)
                    act.sem_inc(waited, 1)
                    with act.If(general):
                        act.activation(k_cur[SHIFT_ROW:P, :], one_row[SHIFT_ROW:P, :].broadcast_to([P - SHIFT_ROW, S]),
                                       ACT.Copy).then_inc(k_made, 1)
                    with act.Else():
                        act.sem_inc(k_made, 1)
                    act.activation(v_cur[:], v_all[:, :, ds(g * HD, HD)], ACT.Copy).then_inc(kv_current, 1)
                    with act.Fori(0, NQ) as qb:
                        F = (b * G + g) * NQ + qb
                        for tt in range(TQ):
                            act.wait_ge(q_turned, F * TQ + tt + 1)
                            act.activation(q_stack[:, :, tt * P:(tt + 1) * P],
                                           S_ps[tt % 2][:].rearrange("p (h n) -> p h n", h=HG), ACT.Copy)\
                                .then_inc(q_stored, 1)
                        with act.If(general):
                            with act.Fori(0, NQUAD) as i:
                                n = F * NQUAD + i
                                act.wait_ge(rows_ready, n + 1)
                                for s in range(2):
                                    act.activation(
                                        q_stack[SHIFT_ROW:SHIFT_ROW + 1, ds(i * QUAD + 2 * s, 2), :]
                                        .rearrange("p h n -> p (h n)"),
                                        S_ps[s][SHIFT_ROW:SHIFT_ROW + 1, :], ACT.Copy).then_inc(shift_stored, 1)
                        with act.Else():
                            act.sem_inc(shift_stored, NQUAD * 2)
                        with act.Fori(0, NQUAD) as i:
                            n = F * NQUAD + i
                            for c in range(NC):
                                for s in range(2):
                                    act.wait_ge(scores_ready, exp_no(n, c, s))
                                    if c >= 2:
                                        act.wait_ge(pv_done, n * NC + c - 1)
                                        m = c - 2 if (c - 2) % SUM else c - 1
                                        act.wait_ge(adds_done, adds_no(n, m, s))
                                    act.activation(expo[:, (2 * c + s) % 4], S_ps[s][:], ACT.Exp, bias=shift[:],
                                                   scale=SCALE)\
                                        .then_inc(exp_done, 1)
                act.wait_ge(att_stored, (b + 1) * (G * NQ * NQUAD) + 1)
                with act.Fori(0, NQ) as qb:
                    for tt in range(TQ):
                        T = b * NT + qb * TQ + tt
                        act.wait_ge(att_projected, T + 1)
                        act.activation(
                            att_tile[:, tt % 2].rearrange("p (g i) n -> p g i n", g=G),
                            q_rot[:].rearrange("p (g q i n) -> p g q i n", g=G, q=NQ, i=NQUAD)
                            [:, :, ds(qb, 1), :, tt * P:(tt + 1) * P].rearrange("p g a i n -> p g (a i) n"),
                            ACT.Copy).then_inc(att_copied, 1)
            with act.Fori(0, T_ALL // 2) as tp:
                for u in range(2):
                    T = tp * 2 + u
                    act.wait_ge(y_turned, T + 3)
                    act.activation(y_t[:, u].rearrange("p k n -> p (k n)"), S_ps[u][:].bitcast(BF16)[:, 0:D],
                                   ACT.Copy).then_inc(yt_stored, 1)
                    act.wait_ge(ffn_done, T + 1)
                    act.wait_ge(final_ready, T + 1)
                    act.activation(ffn_bf[:, u], X_ps[u][:], ACT.Copy, scale=sc[:, 12:13]).then_inc(ffn_scaled, 1)

        @block.tensor
        def _(pe):
            pe.wait_ge(consts_made, 1)
            for c in range(KC):
                pe.wait_ge(w_quantised, c + 1)
                if c >= 2:
                    pe.wait_ge(w_stored, c - 1)
                for k in range(KC):
                    mm = pe.transpose(X_ps[c % 2][:].bitcast(BF16)[:, k * P:(k + 1) * P],
                                      y_q[:, c % 2, k * P:(k + 1) * P], ident_bf[:])
                mm.then_inc(w_turned, 1)
            pe.wait_ge(w_landed, W_ALL)
            with pe.Fori(0, B) as b:
                with pe.Fori(0, NT // 4) as t4:
                    for tt in range(4):
                        u = tt % 2
                        T = b * NT + t4 * 4 + tt
                        pe.wait_ge(xn_ready, T + 1)
                        for k in range(KC):
                            mm = pe.transpose(S_ps[0][:, u * D + k * P:u * D + (k + 1) * P],
                                              xn[:, u, k * P:(k + 1) * P], ident[:])
                        mm.then_inc(xn_turned, 1)
                        pe.wait_ge(xnt_stored, T + 1)
                        pe.wait_ge(proj_read, T + 1)
                        for k in range(KC):
                            pe.matmul(S_ps[1][:, 0:D], xnt[:, u, k, :], w_in[:, k, 0:D],
                                      start=(k == 0), stop=(k == KC - 1))
                            mm = pe.matmul(S_ps[1][:, D:D + KVW], xnt[:, u, k, :], w_in[:, k, D:D + KVW],
                                           start=(k == 0), stop=(k == KC - 1))
                        mm.then_inc(projected, 1)
                    pe.wait_ge(tile_rotated, b * NT + t4 * 4 + 4)
                    pe.wait_ge(k_stored, b * (NT // 2) + t4 * 2 + 2)
                    for t in range(4):
                        for g in range(G):
                            e = (t % 2) * G + g
                            mm = pe.transpose(X_ps[t // 2][:, e * P:(e + 1) * P], k_split[:, t, g, :], ident[:])
                    mm.then_inc(k_turned, 1)
                pe.wait_ge(bound_ready, b + 1)
                pe.sem_inc(waited, 1)
                general = pe.value_load(small[0:1, 0:1], min_val=0, max_val=1) < 1
                with pe.Fori(0, G) as g, pe.Fori(0, NQ) as qb:
                    F = (b * G + g) * NQ + qb
                    for tt in range(TQ):
                        u = tt % 2
                        pe.wait_ge(q_parted, F * TQ + tt + 1)
                        if tt >= 2:
                            pe.wait_ge(q_stored, F * TQ + tt - 1)
                        for h in range(HG):
                            mm = pe.transpose(S_ps[u][:, h * P:(h + 1) * P], q_split[:, u, h, :], ident[:])
                        mm.then_inc(q_turned, 1)
                    def scores(n, i, c, rows, free, ready):
                        for s in range(2):
                            if c:
                                pe.wait_ge(free, exp_no(n, c - 1, s))
                            for j in range(2):
                                mm = pe.matmul(S_ps[s][:, j * QB:(j + 1) * QB],
                                               k_cur[0:rows, c * P:(c + 1) * P],
                                               q_stack[0:rows, ds(i * QUAD + 2 * s + j, 1), :]
                                               .rearrange("p a n -> p (a n)"), start=True, stop=True)
                            mm.then_inc(ready, 1)

                    with pe.If(general):
                        with pe.Fori(0, NQUAD) as i:
                            n = F * NQUAD + i
                            pe.wait_ge(q_stored, F * TQ + TQ)
                            pe.wait_ge(k_made, (b * G + g) + 1)
                            pe.wait_ge(neg_ready, n * 2)
                            for c in range(NC):
                                scores(n, i, c, SHIFT_ROW, pre_maxed, pre_scores)
                            pe.wait_ge(pre_maxed, exp_no(n, NC - 1, 1))
                            for e in range(16):
                                mm = pe.transpose(S_ps[e // 8][:, e % 8 * P:(e % 8 + 1) * P],
                                                  sums[:, e * P:(e + 1) * P], ident[:])
                            mm.then_inc(pre_turned, 1)
                            pe.wait_ge(neg_ready, n * 2 + 2)
                            for e in range(16):
                                mm = pe.transpose(S_ps[e // 8][0:SHIFT_ROW + 1, e % 8 * P:(e % 8 + 1) * P],
                                                  neg_max[:, e:e + SHIFT_ROW + 1], ident[:])
                            mm.then_inc(rows_ready, 1)
                            pe.wait_ge(shift_stored, n * 2 + 2)
                    with pe.Else():
                        pe.sem_inc(pre_scores, NQUAD * 2 * NC)
                        pe.sem_inc(pre_turned, NQUAD)
                        pe.sem_inc(rows_ready, NQUAD)
                    with pe.Fori(0, NQUAD) as i:
                        n = F * NQUAD + i
                        pe.wait_ge(q_stored, F * TQ + TQ)
                        pe.wait_ge(k_made, (b * G + g) + 1)
                        pe.wait_ge(kv_current, (b * G + g) + 1)

                        def weigh(c):
                            pe.wait_ge(exp_done, exp_no(n, c, 1))
                            if c == 0:
                                pe.wait_ge(att_stored, n + 1)
                            for j in range(QUAD):
                                mm = pe.matmul(acc_ps[j * HD:(j + 1) * HD, :], v_cur[:, c, :],
                                               expo[:, (2 * c + j // 2) % 4, j % 2 * QB:(j % 2 + 1) * QB],
                                               start=(c == 0), stop=(c == NC - 1), tile_position=(0, j * HD))
                            mm.then_inc(pv_done, 1)

                        def count(e):
                            pe.wait_ge(adds_done, adds_no(n, e * SUM + SUM - 1, 1))
                            for j in range(QUAD):
                                mm = pe.matmul(den_ps[j * HD:(j + 1) * HD, :], ones[:],
                                               sums[:, j * QB:(j + 1) * QB],
                                               start=(e == 0), stop=(e == NC // SUM - 1), tile_position=(0, j * HD))
                            return mm

                        for c in range(NC):
                            scores(n, i, c, P, exp_done, scores_ready)
                            if c:
                                weigh(c - 1)
                            if c >= SUM + 1 and c % SUM == 1:
                                count(c // SUM - 1).then_inc(sums_used, 1)
                        weigh(NC - 1)
                        count(NC // SUM - 1).then_inc(acc_ready, 1)
                with pe.Fori(0, NT // 2) as tp:
                    for u in range(2):
                        T = b * NT + tp * 2 + u
                        pe.wait_ge(att_copied, T + 1)
                        pe.wait_ge(res_added, T + 1)
                        for k in range(KC):
                            mm = pe.matmul(X_ps[u][:], att_tile[:, u, k, :], w_out[:, k, :],
                                           start=(k == 0), stop=(k == KC - 1))
                        mm.then_inc(att_projected, 1)
            with pe.Fori(0, T_ALL // 2) as tp:
                for u in range(2):
                    T = tp * 2 + u
                    pe.wait_ge(y_ready, T + 1)
                    for k in range(KC):
                        mm = pe.transpose(S_ps[u][:].bitcast(BF16)[:, k * P:(k + 1) * P],
                                          y_q[:, u, k * P:(k + 1) * P], ident_bf[:])
                    mm.then_inc(y_turned, 1)
                    pe.wait_ge(yt_stored, T + 1)
                    pe.wait_ge(ffn_scaled, T + 1)
                    for k in range(KC):
                        mm = pe.matmul(X_ps[u][:], y_t[:, u, k, :], w_ffn_t[:, k, :],
                                       start=(k == 0), stop=(k == KC - 1))
                    mm.then_inc(ffn_done, 1)


def kernel(**inputs):
    import concourse.bacc as bacc
    from concourse.bass_utils import run_bass_kernel_spmd

    names = ["L0_attn_x", "L0_attn_wq", "L0_attn_bq", "L0_attn_wk", "L0_attn_bk", "L0_attn_wv",
             "L0_attn_bv", "L0_attn_wo", "L0_attn_bo", "L0_ffn_weight"]
    arrays = {n: np.ascontiguousarray(inputs[n]) for n in names}
    seq, hd = arrays["L0_attn_x"].shape[1], 32
    inv_freq = np.float32(1.0) / (2500.0 ** (np.arange(0, hd, 2) / hd)).astype(np.float32)
    angle = np.outer(np.arange(seq, dtype=np.float32), inv_freq).astype(np.float32).astype(np.float64)
    arrays["rope_cos"] = np.concatenate([np.cos(angle), np.cos(angle)], -1).astype(np.float32)
    arrays["rope_sin"] = np.concatenate([-np.sin(angle), np.sin(angle)], -1).astype(np.float32)
    nc = bacc.Bacc("TRN2", target_bir_lowering=False, num_devices=1)
    args = [nc.dram_tensor(n, a.shape, mybir.dt.from_np(a.dtype), kind="ExternalInput").ap()
            for n, a in arrays.items()]
    shape = arrays["L0_attn_x"].shape
    result = nc.dram_tensor("result", shape, F32, kind="ExternalOutput").ap()
    layer(nc, *args, result)
    r = run_bass_kernel_spmd(nc, [arrays], core_ids=[0])
    return r.results[0]["result"]
```

```python
from contextlib import ExitStack, contextmanager

import numpy as np

import concourse.bass as bass
from concourse import mybir

F32 = mybir.dt.float32
F32R = mybir.dt.float32r
BF16 = mybir.dt.bfloat16
U32 = mybir.dt.uint32
ALU = mybir.AluOpType
ACT = mybir.ActivationFunctionType
AX = mybir.AxisListType
ds = bass.ds

P = 128
EPS = 1e-5
E4M3_MAX = 448.0


class Steps:

    def __init__(self, eng, sem):
        self.eng, self.sem, self.base, self.k = eng, sem, 0, 0

    def did(self, ins):
        ins.then_inc(self.sem, 1)
        self.k += 1

    def settle(self):
        self.eng.wait_ge(self.sem, self.base + self.k)

    @contextmanager
    def loop(self, count, per):
        base, k = self.base, self.k
        with self.eng.Fori(0, count) as i:
            self.base, self.k = base + k + i * per, 0
            yield i
            assert self.k == per, (self.k, per)
        self.base, self.k = base, k + count * per


def layer(nc, x, wq, bq, wk, bk, wv, bv, wo, bo, w_ffn, rope_cos, rope_sin, out):
    B, S, D = x.shape
    HD = rope_cos.shape[1]
    H, G = wq.shape[1] // HD, wk.shape[1] // HD
    KC = D // P
    NT = S // P
    T_ALL = B * NT
    QB = 512
    NQ = S // QB
    TQ = QB // P
    HG = H // G
    QUAD = P // HD
    NQUAD = HG // QUAD
    NC = S // P
    SUM = 4
    KVW = 2 * G * HD
    QKW = D + G * HD
    NR = QKW // HD
    SHIFT_ROW = 3 * HD
    SCALE = 1.0 / HD
    M_LIMIT = 40.0
    assert KC == 4 and QUAD == 4 and NQUAD == 2 and D == 512 and G == 2

    x_t = x.rearrange("b (t p) d -> p (b t) d", p=P)
    out_t = out.rearrange("b (t p) d -> (b t) p d", p=P)

    with ExitStack() as ctx:
        def sb(name, shape, dt):
            return ctx.enter_context(nc.sbuf_tensor(name, shape, dt))

        def psum(name, shape, dt):
            return ctx.enter_context(nc.psum_tensor(name, shape, dt))

        def sem(name):
            return ctx.enter_context(nc.semaphore(name))

        xs = sb("xs", [P, T_ALL, D], F32)
        w_in = sb("w_in", [P, KC, D + KVW], F32)
        w_out = sb("w_out", [P, KC, D], F32)
        b_in = sb("b_in", [P, D + KVW], F32)
        b_out = sb("b_out", [P, D], F32)
        cos_t = sb("cos_t", [P, NT, HD // 2], F32)
        sin_t = sb("sin_t", [P, NT, HD], F32)
        ident = sb("ident", [P, P], F32)
        ident_bf = sb("ident_bf", [P, P], BF16)
        ones = sb("ones", [P, HD], F32)
        q_rot = sb("q_rot", [P, G * NT * HG * HD], F32)
        k_stack = sb("k_stack", [P, G, S], F32R)
        v_all = sb("v_all", [P, NT, G * HD], F32)
        v_cur = sb("v_cur", [P, NT, HD], F32)
        q_split = sb("q_split", [P, 2, QUAD, P], F32)
        q_stack = sb("q_stack", [P, 2, QUAD, QB], F32R)
        work = sb("work", [P, 10240], F32)
        neg_max = sb("neg_max", [P, SHIFT_ROW + 16], F32)
        stats = sb("stats", [P, T_ALL, 6], F32)
        mom = sb("mom", [P, 8, T_ALL], F32)
        amax = sb("amax", [P, 2, T_ALL], F32)
        norm2 = sb("norm2", [P, NR], F32)
        norm2_max = sb("norm2_max", [P, NR], F32)
        bound = sb("bound", [P, 10], F32)
        shift = sb("shift", [P, 1], F32)
        small = sb("small", [1, 1], mybir.dt.int32)
        one_row = sb("one_row", [P, 1], F32)
        plus_half = sb("plus_half", [P, 2], F32)
        half = sb("half", [P, T_ALL], F32)
        sc = sb("sc", [P, 16], F32)
        spare = sb("spare", [P, 32], F32)

        RING = 4
        expo = work[:, 0:8192].rearrange("p (s n) -> p s n", s=2 * RING)
        sums = [work[:, 8192:10240], w_in[:].rearrange("p k n -> p (k n)")[:, 0:4 * QB]]
        tops = work[:, 0:2048]
        xn = work[:, 0:1024].rearrange("p (u n) -> p u n", u=2)
        xnt = work[:, 1024:2048].rearrange("p (u k n) -> p u k n", u=2, k=KC)
        qk_raw = work[:, 2048:2048 + 2 * QKW].rearrange("p (u n) -> p u n", u=2)
        rot_cos = work[:, 3200:3200 + 2 * QKW].rearrange("p (u n) -> p u n", u=2)
        squares = work[:, 4352:4352 + 2 * QKW].rearrange("p (u n) -> p u n", u=2)
        rot_sin = work[:, 5504:5504 + QKW]
        k_split = work[:, 6144:10240].rearrange("p (t g n) -> p t g n", t=NT, g=G)
        att_tile = work[:, 0:1024].rearrange("p (u k n) -> p u k n", u=2, k=KC)
        y = work[:, 0:1024].rearrange("p (u n) -> p u n", u=2)
        y_pow = work[:, 1024:2048].rearrange("p (u n) -> p u n", u=2)
        y_sum = work[:, 2048:3072].rearrange("p (u n) -> p u n", u=2)
        y_q = work[:, 3072:3584].bitcast(BF16).rearrange("p (u n) -> p u n", u=2)
        y_t = work[:, 3584:4096].bitcast(BF16).rearrange("p (u k n) -> p u k n", u=2, k=KC)
        ffn_bf = work[:, 4096:4608].bitcast(BF16).rearrange("p (u n) -> p u n", u=2)
        w_ffn_rows = work[:, 5120:6144].bitcast(BF16).rearrange("p (c n) -> p c n", c=KC)
        final = work[:, 6144:7168].rearrange("p (u n) -> p u n", u=2)
        w_ffn_t = w_in[:].rearrange("p k n -> p (k n)")[:, 0:KC * D // 2].bitcast(BF16)\
            .rearrange("p (k n) -> p k n", k=KC)

        S_ps = [psum(f"s_ps{i}", [P, 2 * QB], F32) for i in range(2)]
        acc_pair = psum("acc_pair", [P, 2 * QB], F32)
        den_ps = psum("den_ps", [P, QB], F32)
        turn_ps = psum("turn_ps", [P, QB], F32)
        X_ps = [turn_ps, den_ps]
        proj_ps = [S_ps[1], acc_pair]

        x_landed = [sem(f"x_landed{c}") for c in range(4)]
        w_landed = sem("w_landed")
        w_in_landed = sem("w_in_landed")
        w_out_landed = sem("w_out_landed")
        w_ffn_landed = sem("w_ffn_landed")
        pool_step = sem("pool_step")
        dve_step = sem("dve_step")
        act_step = sem("act_step")
        consts_made = sem("consts_made")
        w_amax = sem("w_amax")
        w_amax_all = sem("w_amax_all")
        w_quantised = sem("w_quantised")
        w_turned = sem("w_turned")
        w_stored = sem("w_stored")
        var_ready = sem("var_ready")
        rstd_ready = sem("rstd_ready")
        norm_ready = sem("norm_ready")
        bias_added = sem("bias_added")
        norms_ready = sem("norms_ready")
        norms_all = sem("norms_all")
        root_ready = sem("root_ready")
        bound_ready = sem("bound_ready")
        k_copied = sem("k_copied")
        waited = sem("waited")
        k_made = sem("k_made")
        xn_ready = sem("xn_ready")
        xn_turned = sem("xn_turned")
        xnt_stored = sem("xnt_stored")
        projected = sem("projected")
        proj_read = sem("proj_read")
        qk_ready = sem("qk_ready")
        squared = sem("squared")
        cos_done = sem("cos_done")
        tile_rotated = sem("tile_rotated")
        k_turned = sem("k_turned")
        k_stored = sem("k_stored")
        kv_current = sem("kv_current")
        q_hi = sem("q_hi")
        q_parted = sem("q_parted")
        q_turned = sem("q_turned")
        q_stored = sem("q_stored")
        pre_scores = sem("pre_scores")
        pre_maxed = sem("pre_maxed")
        pre_turned = sem("pre_turned")
        neg_ready = sem("neg_ready")
        rows_ready = sem("rows_ready")
        shift_stored = sem("shift_stored")
        scores_ready = sem("scores_ready")
        exp_done = sem("exp_done")
        pv_done = sem("pv_done")
        adds_done = sem("adds_done")
        sums_used = sem("sums_used")
        acc_ready = sem("acc_ready")
        recip_done = sem("recip_done")
        att_stored = sem("att_stored")
        att_copied = sem("att_copied")
        att_projected = sem("att_projected")
        res_added = sem("res_added")
        y_amax = sem("y_amax")
        y_amax_all = sem("y_amax_all")
        scale_ready = sem("scale_ready")
        y_normed = sem("y_normed")
        y_ready = sem("y_ready")
        y_turned = sem("y_turned")
        yt_stored = sem("yt_stored")
        ffn_done = sem("ffn_done")
        ffn_scaled = sem("ffn_scaled")
        final_ready = sem("final_ready")
        stats_done = sem("stats_done")
        stats2_done = sem("stats2_done")
        out_stored = [sem(f"out_stored{u}") for u in range(2)]
        block = ctx.enter_context(nc.Block())

        QUADS = NQ * NQUAD
        BQ = G * QUADS
        BODY = 8

        def exp_no(n, c, s):
            return n * (2 * NC) + (2 * c + s + 1)

        ADDS = 2 * (SUM - 1)

        def adds_no(n, c, s):
            return n * (NC // SUM * ADDS) + (c // SUM * ADDS + 2 * (max(c % SUM, 1) - 1) + s + 1)

        def built(n, b):
            return (n + b) * TQ + (TQ + 1)

        COUNT_AT = [6, 10, 14]
        TURN_AT = [4, 7, 11, 13]

        def flat(a):
            return a.rearrange("p a n -> p (a n)")

        @block.sync
        def _(sp):
            def load_x(b):
                for c in range(4):
                    t = b * NT + c * (NT // 4)
                    sp.dma_start(xs[:, t:t + NT // 4, :], x_t[:, t:t + NT // 4, :]).then_inc(x_landed[c], 16)

            def load_w_in():
                sp.dma_start(w_in[:, :, 0:D], wq.rearrange("(c p) n -> p c n", p=P)).then_inc(w_in_landed, 16)
                sp.dma_start(w_in[:, :, D:D + G * HD], wk.rearrange("(c p) n -> p c n", p=P))\
                    .then_inc(w_in_landed, 16)
                sp.dma_start(w_in[:, :, D + G * HD:D + KVW], wv.rearrange("(c p) n -> p c n", p=P))\
                    .then_inc(w_in_landed, 16)

            load_x(0)
            load_w_in()
            sp.dma_start(b_in[:, 0:D], bq.partition_broadcast(P)).then_inc(w_landed, 16)
            sp.dma_start(b_in[:, D:D + G * HD], bk.partition_broadcast(P)).then_inc(w_landed, 16)
            sp.dma_start(b_in[:, D + G * HD:D + KVW], bv.partition_broadcast(P)).then_inc(w_landed, 16)
            sp.dma_start(b_out[:], bo.partition_broadcast(P)).then_inc(w_landed, 16)
            sp.dma_start(cos_t[:], rope_cos[:, 0:HD // 2].rearrange("(t p) n -> p t n", p=P)).then_inc(w_landed, 16)
            sp.dma_start(sin_t[:], rope_sin.rearrange("(t p) n -> p t n", p=P)).then_inc(w_landed, 16)
            sp.dma_start(w_out[:], wo.rearrange("(c p) n -> p c n", p=P)).then_inc(w_out_landed, 16)
            for c in range(4):
                sp.wait_ge(x_landed[c], 16)
            load_x(1)
            for b in range(1, B):
                sp.wait_ge(att_stored, b * BQ + 2)
                sp.wait_ge(w_in_landed, b * 48)
                load_w_in()
            sp.wait_ge(att_stored, B * BQ + 2)
            sp.dma_start(w_ffn_rows, w_ffn.rearrange("(c p) n -> p c n", p=P)).then_inc(w_ffn_landed, 16)
            with sp.Fori(0, T_ALL // 2) as tp:
                for u in range(2):
                    sp.wait_ge(final_ready, tp * 2 + u + 3)
                    sp.dma_start(out_t[ds(tp * 2 + u, 1)].rearrange("a p d -> (a p) d"),
                                 final[:, u]).then_inc(out_stored[u], 16)
            for u in range(2):
                sp.wait_ge(out_stored[u], 16 + 16 * (T_ALL // 2))

        @block.gpsimd
        def _(pool):
            step = Steps(pool, pool_step)
            step.did(pool.memset(ident[:], 0.0))
            step.did(pool.memset(half[:], -0.5))
            step.did(pool.memset(plus_half[:], 0.5))
            step.settle()
            step.did(pool.affine_select(out=ident[:], in_=ident[:], compare_op=ALU.not_equal, fill=1.0,
                                        base=0, pattern=[[-1, P]], channel_multiplier=1))
            step.settle()
            pool.tensor_copy(ident_bf[:], ident[:]).then_inc(consts_made, 1)
            pool.wait_ge(w_landed, 16 * 6)

            def part(k, tt, start):
                u = tt % 2
                qs = q_split[:, u].rearrange("p h (s r n) -> p h s r n", s=2, r=2)
                q_new = q_rot[:, ds(start, QUAD * HD)].rearrange("p (h n) -> p h n", h=QUAD)[:, :, None, :]\
                    .broadcast_to([P, QUAD, 2, HD])
                pool.wait_ge(q_turned, k * TQ + tt + 1)
                pool.sem_inc(waited, 1)
                pool.tensor_copy(qs[:, :, 0].bitcast(F32R), q_new).then_inc(q_hi, 1)
                pool.wait_ge(q_hi, k * TQ + tt + 1)
                pool.sem_inc(waited, 1)
                pool.tensor_tensor(qs[:, :, 1], q_new, qs[:, :, 0], ALU.subtract).then_inc(q_parted, 1)

            def build(k, f, quad):
                for tt in range(TQ):
                    part(k, tt, (f * TQ + tt) * (HG * HD) + quad * (QUAD * HD))

            with pool.Fori(0, B) as b:
                pool.wait_ge(var_ready, b + 1)
                pool.tensor_tensor(mom[:, 2, ds(b * NT, NT)], mom[:, 1, ds(b * NT, NT)], half[:, 0:NT], ALU.pow)\
                    .then_inc(rstd_ready, 1)
                pool.wait_ge(rstd_ready, b + 1)
                pool.tensor_tensor(mom[:, 7, ds(b * NT, NT)], mom[:, 0, ds(b * NT, NT)],
                                   mom[:, 2, ds(b * NT, NT)], ALU.mult).then_inc(norm_ready, 1)
                with pool.Fori(0, NT // 2) as tp:
                    for u in range(2):
                        t = tp * 2 + u
                        T = b * NT + t
                        pool.wait_ge(xn_ready, T + 1)
                        tile = xs[:, ds(T, 1), :].rearrange("p a d -> p (a d)")
                        pool.tensor_tensor(tile, tile, b_out[:], ALU.add).then_inc(bias_added, 1)
                        pool.wait_ge(qk_ready, T + 1)
                        pool.wait_ge(tile_rotated, T + 1)
                        pool.tensor_tensor(rot_cos[:, u].rearrange("p (h n) -> p h n", n=HD // 2),
                                           qk_raw[:, u].rearrange("p (h n) -> p h n", n=HD // 2),
                                           cos_t[:, ds(t, 1), :].broadcast_to([P, 2 * NR, HD // 2]), ALU.mult)\
                            .then_inc(cos_done, 1)
                pool.wait_ge(norms_ready, b + 1)
                pool.sem_inc(waited, 1)
                pool.partition_all_reduce(bound[:, 2:4], bound[:, 0:2], P, bass.bass_isa.ReduceOp.max)\
                    .then_inc(norms_all, 1)
                pool.wait_ge(norms_all, b + 1)
                pool.tensor_tensor(bound[:, 4:6], bound[:, 2:4], plus_half[:], ALU.pow).then_inc(root_ready, 1)
                build(b * (BQ + 1), 0, 0)
                with pool.Fori(0, G * NQ) as f:
                    for i in range(NQUAD):
                        n = b * BQ + f * NQUAD + i
                        pool.wait_ge(att_stored, n + 1)
                        build(n + b + 1, f if i == 0 else (f + 1) % (G * NQ), 1 - i)
            pool.wait_ge(w_amax, 1)
            pool.partition_all_reduce(sc[:, 1:2], sc[:, 0:1], P, bass.bass_isa.ReduceOp.max)\
                .then_inc(w_amax_all, 1)
            pool.wait_ge(var_ready, B + 1)
            pool.tensor_tensor(mom[:, 2, :], mom[:, 1, :], half[:], ALU.pow).then_inc(rstd_ready, 1)
            pool.wait_ge(y_amax, 1)
            pool.partition_all_reduce(sc[:, 9:10], sc[:, 8:9], P, bass.bass_isa.ReduceOp.max)\
                .then_inc(y_amax_all, 1)
            with pool.Fori(0, T_ALL // 2) as tp:
                for u in range(2):
                    T = tp * 2 + u
                    pool.wait_ge(ffn_scaled, T + 3)
                    pool.wait_ge(out_stored[u], tp * 16 + 16)
                    pool.tensor_tensor(final[:, u], xs[:, ds(T, 1), :].rearrange("p a d -> p (a d)"),
                                       ffn_bf[:, u], ALU.add).then_inc(final_ready, 1)

        @block.vector
        def _(dve):
            step = Steps(dve, dve_step)

            def quantise(us):
                for u in us:
                    step.did(dve.tensor_scalar(y_pow[:, u].bitcast(U32), y[:, u].bitcast(U32), 0x7F800000, None,
                                               ALU.bitwise_and))
                step.settle()
                for u in us:
                    step.did(dve.tensor_scalar(y_pow[:, u], y_pow[:, u], 2.0 ** -6, 1.5 * 2.0 ** 20,
                                               ALU.max, ALU.mult))
                step.settle()
                for u in us:
                    step.did(dve.tensor_tensor(y_sum[:, u], y[:, u], y_pow[:, u], ALU.add))
                step.settle()
                return [dve.tensor_tensor(y_q[:, u], y_sum[:, u], y_pow[:, u], ALU.subtract) for u in us]

            def scales(col):
                step.did(dve.tensor_scalar(sc[:, col + 1:col + 2], sc[:, col:col + 1], 1.0 / E4M3_MAX, 1e-12,
                                           ALU.mult, ALU.max))
                step.settle()
                step.did(dve.reciprocal(sc[:, col + 2:col + 3], sc[:, col + 1:col + 2]))
                step.settle()

            def moments(first, n):
                st = lambda k: stats[:, ds(first, n), k:k + 1].rearrange("p t a -> p (t a)")
                m = lambda k: mom[:, k, ds(first, n)]
                step.did(dve.tensor_tensor(m(0), st(1), st(4), ALU.add))
                step.did(dve.tensor_tensor(m(3), st(1), st(4), ALU.subtract))
                step.did(dve.tensor_tensor(m(4), st(2), st(5), ALU.add))
                step.settle()
                step.did(dve.tensor_scalar(m(0), m(0), -0.5, None, ALU.mult))
                step.did(dve.tensor_tensor(m(5), m(3), m(3), ALU.mult))
                step.did(dve.tensor_scalar(m(4), m(4), 1.0 / D, EPS, ALU.mult, ALU.add))
                step.settle()
                return dve.scalar_tensor_tensor(out=m(1), in0=m(5), scalar=0.25, in1=m(4),
                                                op0=ALU.mult, op1=ALU.add)

            for k, (signal, n) in enumerate([
                    (proj_read, 2), (projected, 2), (att_stored, 2), (res_added, 2), (xn_turned, 2),
                    (xnt_stored, 2), (tile_rotated, 2), (q_turned, 2), (q_stored, 1), (exp_done, 2),
                    (pv_done, RING), (adds_done, ADDS), (acc_ready, 1), (sums_used, 1), (y_turned, 2), (y_ready, 2),
                    (ffn_scaled, 2), (final_ready, 2), (out_stored[0], 16), (out_stored[1], 16),
                    (k_stored, 2), (att_projected, 2)]):
                dve.memset(spare[:, k:k + 1], 0.0).then_inc(signal, n)
            step.did(dve.memset(ones[:], 1.0))
            step.did(dve.memset(neg_max[:], 0.0))
            step.did(dve.memset(one_row[:], 0.0))
            step.settle()
            step.did(dve.memset(one_row[SHIFT_ROW:SHIFT_ROW + 1, :], 1.0))

            def attention(b, general):
                def find_maxima(p, through):
                    for c in range(NC):
                        for s in range(2):
                            dve.wait_ge(pre_scores, exp_no(p, c, s))
                            top = tops[:, s * 1024:s * 1024 + 1024]
                            if c == 0:
                                dve.wait_ge(adds_done, ADDS + through * (NC // SUM * ADDS))
                                dve.tensor_copy(top, S_ps[s][:]).then_inc(pre_maxed, 1)
                            else:
                                dve.wait_ge(pre_maxed, exp_no(p, c - 1, s))
                                dve.tensor_tensor(top, S_ps[s][:], top, ALU.max).then_inc(pre_maxed, 1)
                    dve.wait_ge(pre_turned, p + 1)
                    for s in range(2):
                        dve.tensor_reduce(neg_max[:, SHIFT_ROW + 8 * s:SHIFT_ROW + 8 * s + 8],
                                          S_ps[s][:].rearrange("p (e n) -> p e n", e=8), AX.X, ALU.max,
                                          negate=True).then_inc(neg_ready, 1)

                def normalise(n, i, place):
                    dve.wait_ge(acc_ready, n + 2)
                    dve.wait_ge(q_parted, (n + b) * TQ + 2 * TQ)
                    dve.reciprocal(place, den_ps[:]).then_inc(recip_done, 1)
                    dve.wait_ge(recip_done, n + 1)
                    dve.tensor_tensor(place, acc_pair[:, i * QB:(i + 1) * QB], place, ALU.mult)\
                        .then_inc(att_stored, 1)

                with dve.Fori(0, G) as g:
                    gg = b * G + g
                    if general:
                        find_maxima(gg * (QUADS + 1), gg * QUADS)
                    with dve.Fori(0, NQ) as qb:
                        for i in range(NQUAD):
                            n = gg * QUADS + qb * NQUAD + i
                            place = lambda k: q_rot[:, ds(((g * NQ + qb) * NQUAD + k) * QB, QB)]
                            for c in range(NC):
                                if c % SUM == 0:
                                    continue
                                for s in range(2):
                                    e = c // SUM
                                    add = sums[e % 2][:, s * 1024:s * 1024 + 1024]
                                    dve.wait_ge(exp_done, exp_no(n, c, s) + 2)
                                    if c % SUM == 1:
                                        if e == 1:
                                            dve.wait_ge(acc_ready, n + 1)
                                        else:
                                            dve.wait_ge(sums_used, n * (NC // SUM - 1) + max(e - 1, 0) + 1)
                                        a = expo[:, (2 * (c - 1) + s) % (2 * RING)]
                                    else:
                                        dve.wait_ge(adds_done, ADDS + adds_no(n, c - 1, s))
                                        a = add
                                    dve.tensor_tensor(add, a, expo[:, (2 * c + s) % (2 * RING)], ALU.add)\
                                        .then_inc(adds_done, 1)
                                if i == 1 and c == 1:
                                    normalise(n - 1, 0, place(0))
                            if general:
                                find_maxima(n + gg + 1, n + 1)
                            if i == 1:
                                normalise(n, 1, place(1))

            BATCH = 6 + 1 + 7 * NT + 5

            def twice(a, h):
                return a[:, :, None, :].broadcast_to([P, h, 2, HD])

            heads = lambda a: a.rearrange("p (h n) -> p h n", n=HD)

            with step.loop(B, BATCH) as b:
                for c in range(4):
                    dve.wait_ge(x_landed[c], b * 16 + 16)
                    dve.sem_inc(waited, 1)
                    with dve.Fori(c * (NT // 4), (c + 1) * (NT // 4)) as t:
                        dve.bn_stats(stats[:, ds(b * NT + t, 1), :].rearrange("p a k -> p (a k)"),
                                     xs[:, ds(b * NT + t, 1), :].rearrange("p a d -> p (a d)"))\
                            .then_inc(stats_done, 1)
                dve.wait_ge(stats_done, b * NT + NT)
                moments(b * NT, NT).then_inc(var_ready, 1)

                step.did(dve.memset(norm2_max[:], 0.0))
                step.settle()
                dve.sem_inc(waited, 1)
                dve.wait_ge(w_landed, 16 * 6)

                def add_bias(tt, t, T):
                    u = tt % 2
                    dve.wait_ge(projected, T + 3)
                    dve.tensor_tensor(qk_raw[:, u], proj_ps[u][:, 0:QKW], b_in[:, 0:QKW], ALU.add)\
                        .then_inc(qk_ready, 1)
                    dve.tensor_tensor(v_all[:, ds(t, 1), :].rearrange("p a n -> p (a n)"),
                                      proj_ps[u][:, QKW:D + KVW], b_in[:, QKW:D + KVW], ALU.add)\
                        .then_inc(proj_read, 1)

                def rotate(tt, t, T):
                    u = tt % 2
                    q = heads(qk_raw[:, u])
                    dve.wait_ge(qk_ready, T + 1)
                    for s in range(2):
                        h0, h1 = s * (HD // 2), (1 - s) * (HD // 2)
                        sin_b = sin_t[:, ds(t, 1), h0:h0 + HD // 2].broadcast_to([P, NR, HD // 2])
                        step.did(dve.tensor_tensor(heads(rot_sin)[:, :, h0:h0 + HD // 2],
                                                   q[:, :, h1:h1 + HD // 2], sin_b, ALU.mult))
                    dve.wait_ge(squared, T + 1)
                    step.did(dve.tensor_reduce(norm2[:, 0:NR], heads(squares[:, u]), AX.X, ALU.add))
                    step.settle()
                    step.did(dve.tensor_tensor(norm2_max[:], norm2_max[:], norm2[:, 0:NR], ALU.max))
                    dve.wait_ge(cos_done, T + 1)
                    k_new = rot_sin[:, D:QKW]
                    step.did(dve.tensor_tensor(k_new, rot_cos[:, u, D:QKW], rot_sin[:, D:QKW], ALU.add))
                    step.did(dve.tensor_tensor(
                        q_rot[:].rearrange("p (g t n) -> p g t n", g=G, t=NT)[:, :, ds(t, 1), :]
                        .rearrange("p g a n -> p g (a n)"),
                        rot_cos[:, u, 0:D].rearrange("p (g n) -> p g n", g=G),
                        rot_sin[:, 0:D].rearrange("p (g n) -> p g n", g=G), ALU.add))
                    step.settle()
                    ks = k_split[:, ds(t, 1)].rearrange("p a g (r s n) -> p (a g) r s n", r=2, s=2)
                    step.did(dve.tensor_copy(ks[:, :, :, 0, :].bitcast(F32R), twice(heads(k_new), G)))
                    step.settle()
                    dve.tensor_tensor(ks[:, :, :, 1, :], twice(heads(k_new), G), ks[:, :, :, 0, :],
                                      ALU.subtract).then_inc(tile_rotated, 1)
                    dve.wait_ge(tile_rotated, T + 3)

                with step.loop(NT // BODY, BODY * 7) as tb:
                    at = lambda tt: (tt, tb * BODY + tt, b * NT + tb * BODY + tt)
                    add_bias(*at(0))
                    for tt in range(1, BODY):
                        add_bias(*at(tt))
                        rotate(*at(tt - 1))
                    rotate(*at(BODY - 1))

                step.settle()
                step.did(dve.tensor_reduce(bound[:, 0:1], norm2_max[:, 0:H], AX.X, ALU.max))
                step.settle()
                dve.tensor_reduce(bound[:, 1:2], norm2_max[:, H:NR], AX.X, ALU.max).then_inc(norms_ready, 1)
                dve.wait_ge(root_ready, b + 1)
                step.did(dve.scalar_tensor_tensor(out=bound[:, 6:7], in0=bound[:, 4:5], scalar=1.001 * SCALE,
                                                  in1=bound[:, 5:6], op0=ALU.mult, op1=ALU.mult))
                step.settle()
                step.did(dve.tensor_scalar(bound[:, 7:8], bound[:, 6:7], M_LIMIT, None, ALU.is_le))
                step.did(dve.tensor_scalar(bound[:, 8:9], bound[:, 6:7], M_LIMIT, -1.0, ALU.min, ALU.mult))
                step.settle()
                step.did(dve.tensor_tensor(shift[:], bound[:, 7:8], bound[:, 8:9], ALU.mult))
                step.settle()
                dve.tensor_copy(small[:], bound[0:1, 7:8]).then_inc(bound_ready, 1)
                dve.wait_ge(bound_ready, b + 1)
                dve.sem_inc(waited, 1)
                general = dve.value_load(small[0:1, 0:1], min_val=0, max_val=1) < 1
                with dve.If(general):
                    attention(b, True)
                with dve.Else():
                    attention(b, False)
                    dve.sem_inc(pre_maxed, G * (QUADS + 1) * 2 * NC)
                    dve.sem_inc(neg_ready, G * (QUADS + 1) * 2)

                with dve.Fori(0, NT // 2) as tp:
                    for u in range(2):
                        T = b * NT + tp * 2 + u
                        tile = lambda: xs[:, ds(T, 1), :].rearrange("p a d -> p (a d)")
                        dve.wait_ge(att_projected, T + 3)
                        dve.wait_ge(bias_added, T + 1)
                        dve.tensor_tensor(tile(), X_ps[u][:], tile(), ALU.add).then_inc(res_added, 1)
                        dve.wait_ge(res_added, T + 3)
                        dve.bn_stats(stats[:, ds(T, 1), :].rearrange("p a k -> p (a k)"), tile()).then_inc(stats2_done, 1)
                        dve.tensor_reduce(amax[:, 0, ds(T, 1)], tile(), AX.X, ALU.max).then_inc(stats2_done, 1)
                        dve.tensor_reduce(amax[:, 1, ds(T, 1)], tile(), AX.X, ALU.min).then_inc(stats2_done, 1)

            dve.wait_ge(w_ffn_landed, 16)
            dve.tensor_reduce(sc[:, 0:1], w_ffn_rows.rearrange("p c n -> p (c n)"), AX.X, ALU.max,
                              apply_absolute_value=True).then_inc(w_amax, 1)
            dve.wait_ge(stats2_done, 3 * T_ALL)
            moments(0, T_ALL).then_inc(var_ready, 1)
            dve.wait_ge(var_ready, B + 1)
            for k in range(2):
                step.did(dve.tensor_tensor(amax[:, k, :], amax[:, k, :], mom[:, 0, :], ALU.add))
            dve.wait_ge(rstd_ready, B + 1)
            step.settle()
            for k in range(2):
                step.did(dve.tensor_tensor(amax[:, k, :], amax[:, k, :], mom[:, 2, :], ALU.mult))
            step.settle()
            dve.tensor_reduce(sc[:, 8:9], amax[:].rearrange("p k t -> p (k t)"), AX.X, ALU.max,
                              apply_absolute_value=True).then_inc(y_amax, 1)
            dve.wait_ge(w_amax_all, 1)
            scales(1)
            for c in range(0, KC, 2):
                for u in range(2):
                    step.did(dve.tensor_scalar(y[:, u], w_ffn_rows[:, c + u, :], sc[:, 3:4], None, ALU.mult))
                step.settle()
                if c:
                    dve.wait_ge(w_turned, c)
                for ins in quantise((0, 1)):
                    ins.then_inc(w_quantised, 1)
                dve.wait_ge(w_quantised, c + 2)
            dve.wait_ge(y_amax_all, 1)
            scales(9)
            step.did(dve.tensor_tensor(sc[:, 12:13], sc[:, 10:11], sc[:, 2:3], ALU.mult))
            step.did(dve.tensor_scalar(mom[:, 6, :], mom[:, 2, :], sc[:, 11:12], None, ALU.mult))
            step.settle()
            dve.tensor_tensor(mom[:, 5, :], mom[:, 0, :], mom[:, 6, :], ALU.mult).then_inc(scale_ready, 1)
            dve.wait_ge(w_turned, KC)
            with step.loop(T_ALL // 2, 2 * 3) as tp:
                dve.wait_ge(y_normed, tp * 2 + 2)
                dve.wait_ge(y_turned, tp * 2 + 2)
                for ins in quantise((0, 1)):
                    ins.then_inc(y_ready, 1)
                dve.wait_ge(y_ready, tp * 2 + 4)

        @block.scalar
        def _(act):
            act.wait_ge(proj_read, 1)
            act.activation(spare[:, 31:32], spare[:, 0:1], ACT.Exp).then_inc(act_step, 1)

            def store_queries(k, tt, i):
                act.wait_ge(q_turned, k + 3)
                act.activation(q_stack[:, i, :, tt * P:(tt + 1) * P],
                               turn_ps[:].rearrange("p (h n) -> p h n", h=QUAD), ACT.Copy).then_inc(q_stored, 1)

            def attention(b, general):
                def store_shift(p, i):
                    act.wait_ge(rows_ready, p + 1)
                    for s in range(2):
                        act.activation(
                            flat(q_stack[SHIFT_ROW:SHIFT_ROW + 1, i, 2 * s:2 * s + 2, :]),
                            S_ps[s][SHIFT_ROW:SHIFT_ROW + 1, :], ACT.Copy).then_inc(shift_stored, 1)

                with act.Fori(0, G) as g:
                    gg = b * G + g
                    act.wait_ge(acc_ready, gg * QUADS + 1)
                    act.activation(k_stack[:, 0, :], flat(k_stack[:, ds(g, 1), :]).bitcast(F32),
                                   ACT.Copy).then_inc(k_copied, 1)
                    if general:
                        act.wait_ge(k_copied, gg + 1)
                        act.activation(k_stack[SHIFT_ROW:P, 0, :],
                                       one_row[SHIFT_ROW:P, :].broadcast_to([P - SHIFT_ROW, S]),
                                       ACT.Copy).then_inc(k_made, 1)
                    act.wait_ge(proj_read, (b + 1) * NT + 2)
                    act.activation(v_cur[:], v_all[:, :, ds(g * HD, HD)], ACT.Copy).then_inc(kv_current, 1)
                    if general:
                        store_shift(gg * (QUADS + 1), 0)
                    with act.Fori(0, NQ) as qb:
                        for i in range(NQUAD):
                            n = gg * QUADS + qb * NQUAD + i
                            for c in range(NC):
                                act.wait_ge(pv_done, n * NC + c + 1)
                                for s in range(2):
                                    act.wait_ge(adds_done, adds_no(n, c, s))
                                    act.wait_ge(scores_ready, gg * 2 + exp_no(n, c, s))
                                    act.activation(expo[:, (2 * c + s) % (2 * RING)], S_ps[s][:], ACT.Exp,
                                                   bias=shift[:], scale=SCALE).then_inc(exp_done, 1)
                                if c in TURN_AT:
                                    tt = TURN_AT.index(c)
                                    store_queries((n + b + 1) * TQ + tt, tt, 1 - i)
                            if general:
                                store_shift(n + gg + 1, 1 - i)

            with act.Fori(0, B) as b:
                def normed(tt, T):
                    u = tt % 2
                    act.wait_ge(xn_turned, T + 1)
                    act.activation(xn[:, u], xs[:, ds(T, 1), :].rearrange("p a d -> p (a d)"), ACT.Identity,
                                   bias=mom[:, 7, ds(T, 1)], scale=mom[:, 2, ds(T, 1)]).then_inc(xn_ready, 1)

                def store_turned(tt, T):
                    u = tt % 2
                    act.wait_ge(xn_turned, T + 3)
                    act.wait_ge(projected, T + 1)
                    act.activation(xnt[:, u].rearrange("p k n -> p (k n)"), S_ps[0][:, u * D:(u + 1) * D],
                                   ACT.Copy).then_inc(xnt_stored, 1)

                def square(tt, T):
                    act.wait_ge(qk_ready, T + 1)
                    act.wait_ge(tile_rotated, T + 1)
                    act.activation(squares[:, tt % 2], qk_raw[:, tt % 2], ACT.Square).then_inc(squared, 1)

                with act.Fori(0, NT // BODY) as tb:
                    at = lambda tt: (tt, b * NT + tb * BODY + tt)
                    act.wait_ge(norm_ready, b + 1)
                    act.wait_ge(att_stored, b * BQ + 2)
                    act.wait_ge(res_added, b * NT + 1)
                    normed(*at(0))
                    for tt in range(1, BODY):
                        normed(*at(tt))
                        store_turned(*at(tt - 1))
                        if tt >= 2:
                            square(*at(tt - 2))
                    store_turned(*at(BODY - 1))
                    square(*at(BODY - 2))
                    square(*at(BODY - 1))
                for r in range(4):
                    act.wait_ge(k_turned, b * 4 + r + 1)
                    act.activation(
                        k_stack[:, :, r * QB:(r + 1) * QB].rearrange("p g (t n) -> p t g n", t=4),
                        S_ps[r % 2][:].rearrange("p (t g n) -> p t g n", t=4, g=G), ACT.Copy)\
                        .then_inc(k_stored, 1)
                for tt in range(TQ):
                    store_queries(b * (BQ + 1) * TQ + tt, tt, 0)
                act.wait_ge(k_stored, b * 4 + 6)
                act.wait_ge(bound_ready, b + 1)
                act.sem_inc(waited, 1)
                general = act.value_load(small[0:1, 0:1], min_val=0, max_val=1) < 1
                with act.If(general):
                    attention(b, True)
                with act.Else():
                    attention(b, False)
                    act.sem_inc(k_made, G)
                    act.sem_inc(shift_stored, G * (QUADS + 1) * 2)
                act.wait_ge(att_stored, (b + 1) * BQ + 2)
                with act.Fori(0, NQ) as qb:
                    for tt in range(TQ):
                        T = b * NT + qb * TQ + tt
                        act.wait_ge(att_projected, T + 1)
                        act.activation(
                            att_tile[:, tt % 2].rearrange("p (g i) n -> p g i n", g=G),
                            q_rot[:].rearrange("p (g q i n) -> p g q i n", g=G, q=NQ, i=NQUAD)
                            [:, :, ds(qb, 1), :, tt * P:(tt + 1) * P].rearrange("p g a i n -> p g (a i) n"),
                            ACT.Copy).then_inc(att_copied, 1)
            for c in range(KC):
                act.wait_ge(w_turned, c + 1)
                act.activation(w_ffn_t[:, :, c * P:(c + 1) * P],
                               X_ps[c % 2][:].bitcast(BF16)[:, 0:D].rearrange("p (k n) -> p k n", k=KC),
                               ACT.Copy).then_inc(w_stored, 1)
            act.wait_ge(scale_ready, 1)
            with act.Fori(0, T_ALL // BODY) as tb:
                def normed2(tt):
                    T, u = tb * BODY + tt, tt % 2
                    act.wait_ge(y_ready, T + 1)
                    act.activation(y[:, u], xs[:, ds(T, 1), :].rearrange("p a d -> p (a d)"), ACT.Identity,
                                   bias=mom[:, 5, ds(T, 1)], scale=mom[:, 6, ds(T, 1)]).then_inc(y_normed, 1)

                def product(tt):
                    T, u = tb * BODY + tt, tt % 2
                    act.wait_ge(y_turned, T + 3)
                    act.activation(y_t[:, u].rearrange("p k n -> p (k n)"), S_ps[u][:].bitcast(BF16)[:, 0:D],
                                   ACT.Copy).then_inc(yt_stored, 1)
                    act.wait_ge(ffn_done, T + 1)
                    act.wait_ge(final_ready, T + 1)
                    act.activation(ffn_bf[:, u], X_ps[u][:], ACT.Copy, scale=sc[:, 12:13]).then_inc(ffn_scaled, 1)

                normed2(0)
                normed2(1)
                for tt in range(2, BODY, 2):
                    normed2(tt)
                    normed2(tt + 1)
                    product(tt - 2)
                    product(tt - 1)
                product(BODY - 2)
                product(BODY - 1)

        @block.tensor
        def _(pe):
            def attention(b, general):
                def scores_of(s, i, c, rows):
                    for j in range(2):
                        mm = pe.matmul(S_ps[s][:, j * QB:(j + 1) * QB], k_stack[0:rows, 0, c * P:(c + 1) * P],
                                       q_stack[0:rows, i, 2 * s + j, :], start=True, stop=True)
                    return mm

                def find_maxima(p, i):
                    for c in range(NC):
                        for s in range(2):
                            if c:
                                pe.wait_ge(pre_maxed, exp_no(p, c - 1, s))
                            scores_of(s, i, c, SHIFT_ROW).then_inc(pre_scores, 1)
                    pe.wait_ge(pre_maxed, exp_no(p, NC - 1, 1))
                    for e in range(16):
                        mm = pe.transpose(S_ps[e // 8][:, e % 8 * P:(e % 8 + 1) * P],
                                          tops[:, e * P:(e + 1) * P], ident[:])
                    mm.then_inc(pre_turned, 1)
                    pe.wait_ge(neg_ready, p * 2 + 2)
                    for e in range(16):
                        mm = pe.transpose(S_ps[e // 8][0:SHIFT_ROW + 1, e % 8 * P:(e % 8 + 1) * P],
                                          neg_max[:, e:e + SHIFT_ROW + 1], ident[:])
                    mm.then_inc(rows_ready, 1)
                    pe.wait_ge(shift_stored, p * 2 + 2)

                def score(n, i, c, s):
                    pe.wait_ge(exp_done, exp_no(n, c, s))
                    scores_of(s, i, c, P).then_inc(scores_ready, 1)

                def weigh(n, i, c):
                    pe.wait_ge(exp_done, exp_no(n, c, 1) + 2)
                    if c == 0:
                        pe.wait_ge(att_stored, n + 1)
                    for j in range(QUAD):
                        mm = pe.matmul(acc_pair[j * HD:(j + 1) * HD, i * QB:(i + 1) * QB], v_cur[:, c, :],
                                       expo[:, (2 * c + j // 2) % (2 * RING), j % 2 * QB:(j % 2 + 1) * QB],
                                       start=(c == 0), stop=(c == NC - 1), tile_position=(0, j * HD))
                    mm.then_inc(pv_done, 1)

                def count(n, e):
                    pe.wait_ge(adds_done, ADDS + adds_no(n, e * SUM + SUM - 1, 1))
                    if e == 0:
                        pe.wait_ge(att_stored, n + 2)
                    for j in range(QUAD):
                        mm = pe.matmul(den_ps[j * HD:(j + 1) * HD, :], ones[:], sums[e % 2][:, j * QB:(j + 1) * QB],
                                       start=(e == 0), stop=(e == NC // SUM - 1), tile_position=(0, j * HD))
                    return mm

                with pe.Fori(0, G) as g:
                    gg = b * G + g
                    first = gg * QUADS
                    pe.wait_ge(q_stored, built(first, b))
                    pe.wait_ge(k_copied, gg + 1)
                    pe.wait_ge(kv_current, gg + 1)
                    if general:
                        pe.wait_ge(exp_done, exp_no(first, 0, 1))
                        pe.sem_inc(waited, 1)
                        pe.wait_ge(k_made, gg + 1)
                        find_maxima(gg * (QUADS + 1), 0)
                    for s in range(2):
                        score(first, 0, 0, s)
                    with pe.Fori(0, NQ) as qb:
                        for i in range(NQUAD):
                            n = first + qb * NQUAD + i
                            for c in range(1, NC):
                                score(n, i, c, 0)
                                if c >= 2:
                                    weigh(n, i, c - 2)
                                score(n, i, c, 1)
                                if c in COUNT_AT:
                                    count(n, COUNT_AT.index(c)).then_inc(sums_used, 1)
                                if c in TURN_AT:
                                    tt = TURN_AT.index(c)
                                    turn_queries((n + b + 1) * TQ + tt, tt)
                            pe.wait_ge(q_stored, built(n + 1, b))
                            if general:
                                pe.wait_ge(exp_done, exp_no(n, NC - 1, 1) + 2)
                                pe.sem_inc(waited, 1)
                                find_maxima(n + gg + 1, 1 - i)
                            score(n + 1, 1 - i, 0, 0)
                            weigh(n, i, NC - 2)
                            score(n + 1, 1 - i, 0, 1)
                            weigh(n, i, NC - 1)
                            count(n, NC // SUM - 1).then_inc(acc_ready, 1)

            def turn_queries(k, tt):
                pe.wait_ge(q_parted, k + 1)
                pe.wait_ge(q_stored, k + 1)
                for h in range(QUAD):
                    mm = pe.transpose(turn_ps[:, h * P:(h + 1) * P], q_split[:, tt % 2, h, :], ident[:])
                mm.then_inc(q_turned, 1)

            pe.wait_ge(consts_made, 1)
            with pe.Fori(0, B) as b:
                def turn(tt, T):
                    u = tt % 2
                    pe.wait_ge(xn_ready, T + 1)
                    pe.wait_ge(xnt_stored, T + 1)
                    for k in range(KC):
                        mm = pe.transpose(S_ps[0][:, u * D + k * P:u * D + (k + 1) * P],
                                          xn[:, u, k * P:(k + 1) * P], ident[:])
                    mm.then_inc(xn_turned, 1)

                def project(tt, T):
                    u = tt % 2
                    pe.wait_ge(xnt_stored, T + 3)
                    pe.wait_ge(proj_read, T + 1)
                    for k in range(KC):
                        pe.matmul(proj_ps[u][:, 0:D], xnt[:, u, k, :], w_in[:, k, 0:D],
                                  start=(k == 0), stop=(k == KC - 1))
                        mm = pe.matmul(proj_ps[u][:, D:D + KVW], xnt[:, u, k, :], w_in[:, k, D:D + KVW],
                                       start=(k == 0), stop=(k == KC - 1))
                    mm.then_inc(projected, 1)

                pe.wait_ge(w_in_landed, (b + 1) * 48)
                pe.sem_inc(waited, 1)
                with pe.Fori(0, NT // BODY) as tb:
                    at = lambda tt: (tt, b * NT + tb * BODY + tt)
                    turn(*at(0))
                    for tt in range(1, BODY):
                        turn(*at(tt))
                        project(*at(tt - 1))
                    project(*at(BODY - 1))
                pe.wait_ge(tile_rotated, (b + 1) * NT + 2)
                pe.sem_inc(waited, 1)
                for r in range(4):
                    pe.wait_ge(k_stored, b * 4 + r + 1)
                    for t in range(4):
                        for g in range(G):
                            e = t * G + g
                            mm = pe.transpose(S_ps[r % 2][:, e * P:(e + 1) * P], k_split[:, 4 * r + t, g, :],
                                              ident[:])
                    mm.then_inc(k_turned, 1)
                for tt in range(TQ):
                    turn_queries(b * (BQ + 1) * TQ + tt, tt)
                pe.wait_ge(bound_ready, b + 1)
                pe.sem_inc(waited, 1)
                general = pe.value_load(small[0:1, 0:1], min_val=0, max_val=1) < 1
                with pe.If(general):
                    attention(b, True)
                with pe.Else():
                    attention(b, False)
                    pe.sem_inc(pre_scores, G * (QUADS + 1) * 2 * NC)
                    pe.sem_inc(pre_turned, G * (QUADS + 1))
                    pe.sem_inc(rows_ready, G * (QUADS + 1))
                pe.wait_ge(w_out_landed, 16)
                with pe.Fori(0, NT // 2) as tp:
                    for u in range(2):
                        T = b * NT + tp * 2 + u
                        pe.wait_ge(att_copied, T + 1)
                        pe.wait_ge(res_added, T + 1)
                        for k in range(KC):
                            mm = pe.matmul(X_ps[u][:], att_tile[:, u, k, :], w_out[:, k, :],
                                           start=(k == 0), stop=(k == KC - 1))
                        mm.then_inc(att_projected, 1)
            for c in range(KC):
                pe.wait_ge(w_quantised, c + 1)
                if c >= 2:
                    pe.wait_ge(w_stored, c - 1)
                for k in range(KC):
                    mm = pe.transpose(X_ps[c % 2][:].bitcast(BF16)[:, k * P:(k + 1) * P],
                                      y_q[:, c % 2, k * P:(k + 1) * P], ident_bf[:])
                mm.then_inc(w_turned, 1)
            pe.wait_ge(w_stored, KC)
            with pe.Fori(0, T_ALL // 2) as tp:
                for u in range(2):
                    T = tp * 2 + u
                    pe.wait_ge(y_ready, T + 3)
                    for k in range(KC):
                        mm = pe.transpose(S_ps[u][:].bitcast(BF16)[:, k * P:(k + 1) * P],
                                          y_q[:, u, k * P:(k + 1) * P], ident_bf[:])
                    mm.then_inc(y_turned, 1)
                    pe.wait_ge(yt_stored, T + 1)
                    pe.wait_ge(ffn_scaled, T + 1)
                    for k in range(KC):
                        mm = pe.matmul(X_ps[u][:], y_t[:, u, k, :], w_ffn_t[:, k, :],
                                       start=(k == 0), stop=(k == KC - 1))
                    mm.then_inc(ffn_done, 1)


def kernel(**inputs):
    import concourse.bacc as bacc
    from concourse.bass_utils import run_bass_kernel_spmd

    names = ["L0_attn_x", "L0_attn_wq", "L0_attn_bq", "L0_attn_wk", "L0_attn_bk", "L0_attn_wv",
             "L0_attn_bv", "L0_attn_wo", "L0_attn_bo", "L0_ffn_weight"]
    arrays = {n: np.ascontiguousarray(inputs[n]) for n in names}
    seq, hd = arrays["L0_attn_x"].shape[1], 32
    inv_freq = np.float32(1.0) / (2500.0 ** (np.arange(0, hd, 2) / hd)).astype(np.float32)
    angle = np.outer(np.arange(seq, dtype=np.float32), inv_freq).astype(np.float32).astype(np.float64)
    arrays["rope_cos"] = np.concatenate([np.cos(angle), np.cos(angle)], -1).astype(np.float32)
    arrays["rope_sin"] = np.concatenate([-np.sin(angle), np.sin(angle)], -1).astype(np.float32)
    nc = bacc.Bacc("TRN2", target_bir_lowering=False, num_devices=1)
    args = [nc.dram_tensor(n, a.shape, mybir.dt.from_np(a.dtype), kind="ExternalInput").ap()
            for n, a in arrays.items()]
    shape = arrays["L0_attn_x"].shape
    result = nc.dram_tensor("result", shape, F32, kind="ExternalOutput").ap()
    layer(nc, *args, result)
    r = run_bass_kernel_spmd(nc, [arrays], core_ids=[0])
    return r.results[0]["result"]
```
